# Optimizing a Trainium2 kernel written in Bass

```python
import numpy as np
import jax
import jax.numpy as jnp

def _softmax(x, axis=-1):
    return jax.nn.softmax(x, axis=axis)
def _gelu(x):
    return jax.nn.gelu(x, approximate=True)
def _silu(x):
    return jax.nn.silu(x)
def _sigmoid(x):
    return jax.nn.sigmoid(x)
def _layernorm(x, axis=-1, eps=1e-5):
    m = jnp.mean(x, axis=axis, keepdims=True)
    v = jnp.var(x, axis=axis, keepdims=True)
    return (x - m) / jnp.sqrt(v + eps)
def _scatter_add(tgt, idx, src, axis=0):
    return tgt.at[idx].add(src)
def _segment_sum(src, seg, n):
    return jax.ops.segment_sum(src, seg, n)

kernel_name = 'mk_conv_seq_d1_conv_nhwc256_f00ea6'

def setup_inputs(seed: int = 0):
    np.random.seed(seed)
    _w = jnp.asarray
    def _rec_inputs():
        import jax
        import jax.numpy as jnp
        _gk = jax.random.key(seed)
        x = -0.0003929 + 0.9999 * jax.random.normal(jax.random.fold_in(_gk, 1), (16, 64, 64, 256), jnp.float32)
        return x
    x = _rec_inputs()
    def _L0_conv_setup():
        import jax, jax.numpy as jnp
        import numpy as np
        NUM_HEADS = 8
        KERNEL = 3

        def _arsinh_norm(x, w, b):
            return w * jnp.arcsinh(x) + b

        def _nbr_idx(L, k):
            start = jnp.clip(jnp.arange(L) - k // 2, 0, L - k)
            return start[:, None] + jnp.arange(k)

        def _na2d(x, qkv_w, qkv_b, proj_w, proj_b, num_heads=NUM_HEADS, k=KERNEL):
            B, H, W, C = x.shape
            hd = C // num_heads
            qkv = x @ qkv_w + qkv_b
            q, kk, v = jnp.split(qkv, 3, axis=-1)
            q = q.reshape(B, H, W, num_heads, hd) * hd ** (-0.5)
            kk = kk.reshape(B, H, W, num_heads, hd)
            v = v.reshape(B, H, W, num_heads, hd)
            ri = _nbr_idx(H, k)[:, None, :, None]
            ci = _nbr_idx(W, k)[None, :, None, :]
            nb_k = kk[:, ri, ci].reshape(B, H, W, k * k, num_heads, hd)
            nb_v = v[:, ri, ci].reshape(B, H, W, k * k, num_heads, hd)
            scores = jnp.einsum('bijnd,bijmnd->bijnm', q, nb_k)
            attn = jax.nn.softmax(scores, axis=-1)
            out = jnp.einsum('bijnm,bijmnd->bijnd', attn, nb_v).reshape(B, H, W, C)
            return out @ proj_w + proj_b
        key = jax.random.key(seed)
        ks = jax.random.split(key, 8)
        B, H, W, C = (16, 64, 64, 256)
        s = 0.02
        return {'h': jax.random.normal(ks[0], (B, H, W, C), dtype=jnp.float32), 'qkv_w': jax.random.normal(ks[1], (C, 3 * C), dtype=jnp.float32) * s, 'qkv_b': jnp.zeros((3 * C,), jnp.float32), 'proj_w': jax.random.normal(ks[2], (C, C), dtype=jnp.float32) * s, 'proj_b': jnp.zeros((C,), jnp.float32), 'n1_w': jnp.ones((C,), jnp.float32), 'n1_b': jnp.zeros((C,), jnp.float32), 'n2_w': jnp.ones((C,), jnp.float32), 'n2_b': jnp.zeros((C,), jnp.float32), 'mlp_w1': jax.random.normal(ks[3], (C, 2 * C), dtype=jnp.float32) * s, 'mlp_b1': jnp.zeros((2 * C,), jnp.float32), 'mlp_w2': jax.random.normal(ks[4], (2 * C, C), dtype=jnp.float32) * s, 'mlp_b2': jnp.zeros((C,), jnp.float32)}
    _L0_conv_all = _L0_conv_setup()
    _L0_conv_in = {k: v for k, v in _L0_conv_all.items() if k in ('qkv_w', 'qkv_b', 'proj_w', 'proj_b', 'n1_w', 'n1_b', 'n2_w', 'n2_b', 'mlp_w1', 'mlp_b1', 'mlp_w2', 'mlp_b2', )}
    del _L0_conv_all

    return {
        "x": x,
        "L0_conv_qkv_w": _L0_conv_in["qkv_w"],
        "L0_conv_qkv_b": _L0_conv_in["qkv_b"],
        "L0_conv_proj_w": _L0_conv_in["proj_w"],
        "L0_conv_proj_b": _L0_conv_in["proj_b"],
        "L0_conv_n1_w": _L0_conv_in["n1_w"],
        "L0_conv_n1_b": _L0_conv_in["n1_b"],
        "L0_conv_n2_w": _L0_conv_in["n2_w"],
        "L0_conv_n2_b": _L0_conv_in["n2_b"],
        "L0_conv_mlp_w1": _L0_conv_in["mlp_w1"],
        "L0_conv_mlp_b1": _L0_conv_in["mlp_b1"],
        "L0_conv_mlp_w2": _L0_conv_in["mlp_w2"],
        "L0_conv_mlp_b2": _L0_conv_in["mlp_b2"],
    }

def reference(x, L0_conv_qkv_w, L0_conv_qkv_b, L0_conv_proj_w, L0_conv_proj_b, L0_conv_n1_w, L0_conv_n1_b, L0_conv_n2_w, L0_conv_n2_b, L0_conv_mlp_w1, L0_conv_mlp_b1, L0_conv_mlp_w2, L0_conv_mlp_b2):
    import jax
    import jax.numpy as jnp
    def _L0_conv_ref(h, qkv_w, qkv_b, proj_w, proj_b, n1_w, n1_b, n2_w, n2_b, mlp_w1, mlp_b1, mlp_w2, mlp_b2):
        import jax, jax.numpy as jnp
        import numpy as np
        NUM_HEADS = 8
        KERNEL = 3

        def _arsinh_norm(x, w, b):
            return w * jnp.arcsinh(x) + b

        def _nbr_idx(L, k):
            start = jnp.clip(jnp.arange(L) - k // 2, 0, L - k)
            return start[:, None] + jnp.arange(k)

        def _na2d(x, qkv_w, qkv_b, proj_w, proj_b, num_heads=NUM_HEADS, k=KERNEL):
            B, H, W, C = x.shape
            hd = C // num_heads
            qkv = x @ qkv_w + qkv_b
            q, kk, v = jnp.split(qkv, 3, axis=-1)
            q = q.reshape(B, H, W, num_heads, hd) * hd ** (-0.5)
            kk = kk.reshape(B, H, W, num_heads, hd)
            v = v.reshape(B, H, W, num_heads, hd)
            ri = _nbr_idx(H, k)[:, None, :, None]
            ci = _nbr_idx(W, k)[None, :, None, :]
            nb_k = kk[:, ri, ci].reshape(B, H, W, k * k, num_heads, hd)
            nb_v = v[:, ri, ci].reshape(B, H, W, k * k, num_heads, hd)
            scores = jnp.einsum('bijnd,bijmnd->bijnm', q, nb_k)
            attn = jax.nn.softmax(scores, axis=-1)
            out = jnp.einsum('bijnm,bijmnd->bijnd', attn, nb_v).reshape(B, H, W, C)
            return out @ proj_w + proj_b
        h1 = _arsinh_norm(h, n1_w, n1_b)
        h = h + _na2d(h1, qkv_w, qkv_b, proj_w, proj_b)
        h2 = _arsinh_norm(h, n2_w, n2_b)
        ff = jax.nn.gelu(h2 @ mlp_w1 + mlp_b1, approximate=False) @ mlp_w2 + mlp_b2
        return h + ff

    def _gn(v, G=32, eps=1e-5):
        B_, H_, W_, C_ = v.shape
        g = v.reshape(B_, H_, W_, G, C_ // G)
        m = jnp.mean(g, axis=(1, 2, 4), keepdims=True)
        s = jnp.var(g, axis=(1, 2, 4), keepdims=True)
        return ((g - m) / jnp.sqrt(s + eps)).reshape(v.shape)

    def _ln_c(v, eps=1e-6):
        m = jnp.mean(v, axis=-1, keepdims=True)
        s = jnp.var(v, axis=-1, keepdims=True)
        return (v - m) / jnp.sqrt(s + eps)

    def _ln_t(v, eps=1e-5):
        m = jnp.mean(v, axis=-1, keepdims=True)
        s = jnp.var(v, axis=-1, keepdims=True)
        return (v - m) / jnp.sqrt(s + eps)

    def _to_tokens(v):
        B_, H_, W_, C_ = v.shape
        return v.reshape(B_, H_ * W_, C_)
    def _from_tokens(t, like):
        return t.reshape(like.shape)

    x = _L0_conv_ref(x, L0_conv_qkv_w, L0_conv_qkv_b, L0_conv_proj_w, L0_conv_proj_b, L0_conv_n1_w, L0_conv_n1_b, L0_conv_n2_w, L0_conv_n2_b, L0_conv_mlp_w1, L0_conv_mlp_b1, L0_conv_mlp_w2, L0_conv_mlp_b2)
    return x


_drawn_inputs = setup_inputs


def setup_inputs(seed=0):
    import zlib

    import numpy as np

    out = dict(_drawn_inputs(seed))
    spreads = {'L0_conv_qkv_b': (0.0, 0.1),
     'L0_conv_proj_b': (0.0, 0.1),
     'L0_conv_n1_w': (1.0, 0.6),
     'L0_conv_n1_b': (0.0, 0.779),
     'L0_conv_n2_w': (1.0, 0.6),
     'L0_conv_n2_b': (0.0, 0.8),
     'L0_conv_mlp_b1': (0.0, 0.351),
     'L0_conv_mlp_b2': (0.0, 0.1)}
    factors = {}
    for name, (base, spread) in spreads.items():
        noise = np.random.default_rng([zlib.crc32(name.encode()), seed]).standard_normal(out[name].shape)
        drawn = base * np.exp(spread * noise) if base else spread * noise
        out[name] = jnp.asarray(drawn.astype(out[name].dtype))
    for name, factor in factors.items():
        out[name] = (out[name] * factor).astype(out[name].dtype)
    return out
```

```python
from contextlib import ExitStack

import numpy as np

import concourse.bass as bass
from concourse import mybir

ALU = mybir.AluOpType
ACT = mybir.ActivationFunctionType
F32 = mybir.dt.float32
F16 = mybir.dt.float16
U32 = mybir.dt.uint32
AX = mybir.AxisListType

P = 128
IMAGES, SIDE, C = 16, 64, 256
HEADS = 8
HD = C // HEADS
HID = 2 * C
G = C // P
PAIRS = HEADS // 2
TS = 8
WIN = TS + 2
NK = WIN * WIN
NQ = TS * TS
TILES = SIDE // TS
BPI = SIDE // TS
BANDS = IMAGES * BPI
TOK = TS * SIDE
XROWS = WIN
XTOK = XROWS * SIDE
PITCH = SIDE + 2
PADTOK = XROWS * PITCH
HALF = TILES // 2 * NK
VW = 2 * HD + 1
MT = HID // P
WS = 64.0
INV = 1.0 / WS
M0 = 32
MASKED_Q, MASKED_K = -32768.0, 256.0
SIGN, MAGNITUDE = 0x80000000, 0x7FFFFFFF

N_LOADS = 16 + 2 * PAIRS
N_ZERO = 16
V_BV, V_ALL = 1, 29

B_S, B_ST, B_V, B_AV, B_OT = 2, 3, 5, 6, 7


def constants():
    ident = np.eye(P, dtype=np.float32)
    ident_ws = np.eye(P, dtype=np.float32) * np.float32(WS)
    marks = np.zeros((P, WIN, WIN), np.float16)
    for r in range(WIN):
        marks[r, r, :] = MASKED_K
        marks[WIN + r, :, r] = MASKED_K
    marks = marks.reshape(P, 1, NK)
    key_scores = np.repeat(marks, PAIRS, axis=1)
    key_probs = key_scores.copy()
    for p in range(PAIRS):
        key_probs[M0 + p, p, :] = -1.0
    query = np.zeros((BPI, 2 * WIN, TILES, 2, TS, TS), np.float16)
    for b in range(BPI):
        for q in range(TS):
            first = min(max(TS * b + q - 1, 0), SIDE - 3)
            for r in range(WIN):
                if not first <= TS * b - 1 + r < first + 3:
                    query[b, r, :, :, q, :] = MASKED_Q
    for c in range(TILES):
        for q in range(TS):
            first = min(max(TS * c + q - 1, 0), SIDE - 3)
            for r in range(WIN):
                if not first <= TS * c - 1 + r < first + 3:
                    query[:, WIN + r, c, :, :, q] = MASKED_Q
    return {
        "ident": ident,
        "ident_ws": ident_ws,
        "ident16": np.eye(P, dtype=np.float16),
        "key_scores": key_scores.reshape(P, PAIRS * NK),
        "key_probs": key_probs.reshape(P, PAIRS * NK),
        "query_mask": query.reshape(BPI, 2 * WIN, TILES * P),
    }


def build(nc, x, qkv_w, qkv_b, proj_w, proj_b, n1_w, n1_b, n2_w, n2_b, mlp_w1, mlp_b1, mlp_w2, mlp_b2,
          ident_c, ident_ws_c, ident16_c, key_scores_c, key_probs_c, query_mask_c, out):
    x_rows = x.rearrange("i r j c -> (i r j) c")
    out_rows = out.rearrange("i r j c -> (i r j) c")

    with ExitStack() as ctx:
        def sb(name, shape, dt):
            return ctx.enter_context(nc.sbuf_tensor(name, shape, dt))

        def sem(name):
            return ctx.enter_context(nc.semaphore(name))

        ps = ctx.enter_context(nc.psum_tensor("ps", [P, 8, 512], F32))

        ident = sb("ident", [P, P], F32)
        ident_ws = sb("ident_ws", [P, P], F32)
        ident16 = sb("ident16", [P, P], F16)
        key_scores = sb("key_scores", [P, PAIRS, NK], F16)
        key_probs = sb("key_probs", [P, PAIRS, NK], F16)
        ones16 = sb("ones16", [P, TOK], F16)
        wqkv = sb("wqkv", [P, G, 3 * C], F32)
        wproj = sb("wproj", [P, 2, C], F32)
        w1 = sb("w1", [P, G, HID], F32)
        w2 = sb("w2", [P, MT, C], F32)
        wqkv_hi, wqkv_lo = sb("wqkv_hi", [P, G, 3 * C], F16), sb("wqkv_lo", [P, G, 3 * C], F16)
        wproj_hi, wproj_lo = sb("wproj_hi", [P, 2, C], F16), sb("wproj_lo", [P, 2, C], F16)
        w1_hi, w1_lo = sb("w1_hi", [P, G, HID], F16), sb("w1_lo", [P, G, HID], F16)
        w2_hi, w2_lo = sb("w2_hi", [P, MT, C], F16), sb("w2_lo", [P, MT, C], F16)
        n1w, n1b = sb("n1w", [P, G], F32), sb("n1b", [P, G], F32)
        n2w, n2b = sb("n2w", [P, G], F32), sb("n2b", [P, G], F32)
        bv_in, bv = sb("bv_in", [P, 2], F32), sb("bv", [P, 2], F32)
        b1_in, b1 = sb("b1_in", [P, MT], F32), sb("b1", [P, MT], F32)
        bias = sb("bias", [P, 4 * C], F16)

        xin = [sb(f"xin{i}", [P, XTOK // P, C], F32) for i in range(2)]
        xT = [sb(f"xT{i}", [P, G, XROWS, PITCH], F32) for i in range(2)]
        a_hi = [sb(f"a_hi{i}", [P, G, TILES, NK], F16) for i in range(2)]
        a_lo = [sb(f"a_lo{i}", [P, G, TILES, NK], F16) for i in range(2)]
        k_hi = [sb(f"k_hi{i}", [P, G, TILES, NK], F16) for i in range(2)]
        k_lo = [sb(f"k_lo{i}", [P, G, TILES, NK], F16) for i in range(2)]
        q_hi = [sb(f"q_hi{i}", [P, G, TILES, 4, NQ], F16) for i in range(2)]
        q_lo = [sb(f"q_lo{i}", [P, G, TILES, 4, NQ], F16) for i in range(2)]
        qmask = [sb(f"qmask{i}", [P, TILES, P], F16) for i in range(2)]
        o_hi = [sb(f"o_hi{i}", [P, 2, TOK], F16) for i in range(2)]
        o_lo = [sb(f"o_lo{i}", [P, 2, TOK], F16) for i in range(2)]
        v_hi = [sb(f"v_hi{i}", [P, PAIRS, VW], F16) for i in range(2)]
        v_lo = [sb(f"v_lo{i}", [P, PAIRS, VW], F16) for i in range(2)]
        prob = [sb(f"prob{i}", [P, 512], F32) for i in range(2)]
        p_hi = [sb(f"p_hi{i}", [P, 512], F16) for i in range(2)]
        p_lo = [sb(f"p_lo{i}", [P, 512], F16) for i in range(2)]
        maxima = [sb(f"maxima{i}", [P, P], F16) for i in range(2)]
        recip = [sb(f"recip{i}", [P, PAIRS, 1], F32) for i in range(2)]
        o_norm = [sb(f"o_norm{i}", [P, PAIRS, HD], F32) for i in range(2)]
        ln1_s, ln1_u = sb("ln1_s", [P, G * PADTOK], F32), sb("ln1_u", [P, G * PADTOK], F32)
        ln2_s, ln2_u = sb("ln2_s", [P, G * TOK], F32), sb("ln2_u", [P, G * TOK], F32)
        h = sb("h", [P, G, TOK], F32)
        b_hi, b_lo = sb("b_hi", [P, G, TOK], F16), sb("b_lo", [P, G, TOK], F16)
        g32 = sb("g32", [P, MT, TOK], F32)
        g_hi, g_lo = sb("g_hi", [P, MT, TOK], F16), sb("g_lo", [P, MT, TOK], F16)
        y = [sb(f"y{i}", [P, 2, C], F32) for i in range(2)]
        wscaled = sb("wscaled", [P, G * 3 * C], F32)
        brow_in = g32[0:1, 0:2, :].rearrange("p m n -> p (m n)")
        brow = g32[0:1, 2:4, :].rearrange("p m n -> p (m n)")
        brow16 = g_hi[0:1, 0:2, :].rearrange("p m n -> p (m n)")

        w_in = sem("w_in")
        x_in = [sem("x_in0"), sem("x_in1")]
        edge_in = sem("edge_in")
        mask_in = [sem("mask_in0"), sem("mask_in1")]
        y_out = [sem("y_out0"), sem("y_out1")]
        zeroed, setup_v, setup_pe = sem("zeroed"), sem("setup_v"), sem("setup_pe")
        pe_x, pe_q, pe_k, pe_proj, pe_m1, pe_m2 = (sem("pe_" + s) for s in ("x", "q", "k", "proj", "m1", "m2"))
        pe_s, pe_v, pe_max, pe_st, pe_av, pe_ot = (sem("pe_" + s) for s in ("s", "v", "max", "st", "av", "ot"))
        xT_ready, h_ready, abs1, abs2, sum1, sum2 = (sem("dve_" + s) for s in ("xT", "h", "abs1", "abs2", "sum1", "sum2"))
        asinh1, asinh2, a_hi_ready, b_hi_ready = (sem("dve_" + s) for s in ("asinh1", "asinh2", "a_hi", "b_hi"))
        q_lo_ready, k_lo_ready, g_hi_ready = (sem("dve_" + s) for s in ("q_lo", "k_lo", "g_hi"))
        max_ready, v_lo_ready, maxrow_ready = (sem("dve_" + s) for s in ("max", "v_lo", "maxrow"))
        recip_ready, norm_ready, o_lo_ready = (sem("dve_" + s) for s in ("recip", "norm", "o_lo"))
        sq1, ln1a, root1, log1, sq2, ln2a, root2, log2 = (
            sem("act_" + s) for s in ("sq1", "ln1a", "root1", "log1", "sq2", "ln2a", "root2", "log2"))
        q_hi_ready, k_hi_ready, gelu_ready, y_ready = (sem("act_" + s) for s in ("q_hi", "k_hi", "gelu", "y"))
        v_hi_ready, prob_ready, p_hi_ready, o_hi_ready = (sem("act_" + s) for s in ("v_hi", "prob", "p_hi", "o_hi"))
        a_lo_ready, b_lo_ready, g_lo_ready, p_lo_ready = (sem("pool_" + s) for s in ("a_lo", "b_lo", "g_lo", "p_lo"))

        block = ctx.enter_context(nc.Block())

        def flat(t):
            return t[:].rearrange("p g r c -> p (g r c)")

        def flat2(t):
            return t[:].rearrange("p g n -> p (g n)")

        def o_tile(o, c):
            return o[:].rearrange("p e (i c j) -> p e c i j", c=TILES, j=TS)[:, :, c % TILES]

        def ps_ot():
            return ps[:, B_OT, 0:P].rearrange("p (e i j) -> p e i j", e=2, j=TS)

        def exists(t, c):
            return not isinstance(t, int) or 0 <= TILES * t + c < TILES * BANDS

        def signals(t, per, n):
            return max(t * per + n, 0) if isinstance(t, int) else t * per + n

        def run(eng, step):
            step(-1, 1, False, True, False)
            step(0, 0, True, True, False)
            with eng.Fori(0, (BANDS - 2) // 2) as i:
                step(i * 2 + 1, 1, True, True, True)
                step(i * 2 + 2, 0, True, True, True)
            step(BANDS - 1, 1, True, False, True)
            step(BANDS, 0, False, False, True)

        def window(t, g, c):
            return t[:, g, c, :]

        def keys(t, g, half):
            return t[:, g].rearrange("p c k -> p (c k)")[:, half * HALF:(half + 1) * HALF]

        def by_window(t, g):
            return t[:, g].rearrange("p c (r j) -> p c r j", j=WIN)

        def in_windows(u, g):
            a = u[:, g * PADTOK:(g + 1) * PADTOK]
            return bass.AP(a.tensor, a.offset, [list(a.ap[0]), [TS, TILES], [PITCH, WIN], [1, WIN]])

        @block.sync
        def _(sp):
            loads = [
                (ident[:], ident_c), (ident_ws[:], ident_ws_c), (ident16[:], ident16_c),
                (key_scores[:].rearrange("p a k -> p (a k)"), key_scores_c),
                (key_probs[:].rearrange("p a k -> p (a k)"), key_probs_c),
                (wqkv[:], qkv_w.rearrange("(g p) n -> p g n", p=P)),
                (w1[:], mlp_w1.rearrange("(g p) n -> p g n", p=P)),
                (w2[:], mlp_w2.rearrange("(m p) n -> p m n", p=P)),
                (n1w[:], n1_w.rearrange("(g p) -> p g", p=P)), (n1b[:], n1_b.rearrange("(g p) -> p g", p=P)),
                (n2w[:], n2_w.rearrange("(g p) -> p g", p=P)), (n2b[:], n2_b.rearrange("(g p) -> p g", p=P)),
                (b1_in[:], mlp_b1.rearrange("(m p) -> p m", p=P)),
                (brow_in[:, 0:2 * C], qkv_b[0:2 * C].rearrange("(a n) -> a n", a=1)),
                (brow_in[:, 2 * C:3 * C], proj_b.rearrange("(a n) -> a n", a=1)),
                (brow_in[:, 3 * C:4 * C], mlp_b2.rearrange("(a n) -> a n", a=1)),
            ]
            wp = proj_w.rearrange("(p e d) n -> p d e n", p=PAIRS, e=2)
            bvp = qkv_b[2 * C:3 * C].rearrange("(p e d) -> p d e", p=PAIRS, e=2)
            for p in range(PAIRS):
                loads.append((wproj[HD * p:HD * p + HD], wp[p]))
                loads.append((bv_in[HD * p:HD * p + HD], bvp[p]))
            assert len(loads) == N_LOADS
            for to, of in loads:
                sp.dma_start(to, of, allow_slow_non_contiguous=True).then_inc(w_in, 16)

            def load_x(t, par):
                sp.dma_start(xin[par][:], x_rows[bass.ds(t * TOK - SIDE, XTOK)].rearrange("(k p) c -> p k c", p=P)
                             ).then_inc(x_in[par], 16)

            def load_edge_x(t, par):
                above = t == 0
                beyond = 0 if above else XROWS - 1
                tiles = slice(1, XTOK // P) if above else slice(0, XTOK // P - 1)
                beside = 1 if above else XROWS - 2
                edge = t * TOK if above else (t + 1) * TOK - SIDE
                for slot in (beyond, beside):
                    at = slot * SIDE
                    sp.dma_start(xin[par][at % P:at % P + SIDE, at // P, :], x_rows[edge:edge + SIDE]).then_inc(edge_in, 16)
                sp.wait_ge(edge_in, 32 if above else 64)
                first = t * TOK - SIDE + tiles.start * P
                sp.dma_start(xin[par][:, tiles, :], x_rows[first:first + 4 * P].rearrange("(k p) c -> p k c", p=P)
                             ).then_inc(x_in[par], 16)

            def load_mask(t, par, b):
                sp.dma_start(qmask[par][0:2 * WIN].rearrange("k c q -> k (c q)"), query_mask_c[b]).then_inc(mask_in[par], 16)

            def store_y(t, par):
                for n in range(2):
                    sp.wait_ge(y_ready, signals(t, 2, n + 1))
                    dst = out_rows[bass.ds(t * TOK + n * 2 * P, 2 * P)]
                    sp.dma_start(dst.rearrange("(k p) c -> p k c", p=P), y[n][:]).then_inc(y_out[n], 16)

            sp.wait_ge(zeroed, N_ZERO)
            load_edge_x(0, 0)
            load_mask(0, 0, 0)
            load_x(1, 1)
            load_mask(1, 1, 1)

            def step(t, par):
                sp.wait_ge(pe_x, signals(t, 4, 0))
                load_x(t + 1, 1 - par)
                sp.wait_ge(pe_st, signals(t, TILES, 0))
                load_mask(t + 1, 1 - par, (t + 1) % BPI)
                store_y(t - 1, 1 - par)

            with sp.Fori(0, (BANDS - 4) // 2) as i:
                step(i * 2 + 1, 1)
                step(i * 2 + 2, 0)
            step(BANDS - 3, 1)
            sp.wait_ge(pe_x, signals(BANDS - 2, 4, 0))
            load_edge_x(BANDS - 1, 1)
            sp.wait_ge(pe_st, signals(BANDS - 2, TILES, 0))
            load_mask(BANDS - 1, 1, BPI - 1)
            for t in range(BANDS - 3, BANDS):
                store_y(t, t % 2)
            for n in range(2):
                sp.wait_ge(y_out[n], 16 * BANDS)

        def x_count(t, par):
            return (t // 2) * 16 + 16

        def mask_count(t, par):
            return (t // 2) * 16 + 16

        @block.tensor
        def _(pe):
            D = [ps[:, 0, :], ps[:, 1, :]]

            def mm(o, a, b, start=False, stop=False):
                return pe.matmul(o, a, b, start=start, stop=stop, skip_group_check=True)

            def three(o, a_parts, b_parts, start, stop):
                (ah, al), (bh, bl) = a_parts, b_parts
                mm(o, ah, bh, start=start)
                mm(o, ah, bl)
                return mm(o, al, bh, stop=stop)

            pe.wait_ge(w_in, 16 * N_LOADS)
            pe.wait_ge(zeroed, N_ZERO)
            for g in range(G):
                mm(ps[0:1, 0, :], n1b[:, g:g + 1], wqkv[:, g, 0:2 * C], start=(g == 0), stop=(g == 1))
            for e in range(2):
                for p in range(PAIRS):
                    for g in range(G):
                        a = 2 * C + (2 * p + e) * HD
                        mm(ps[HD * p:HD * p + HD, 1 + e, 0:1], wqkv[:, g, a:a + HD], n1b[:, g:g + 1],
                           start=(g == 0), stop=(g == 1))
            for m in range(MT):
                for g in range(G):
                    s = mm(ps[:, 3, m:m + 1], w1[:, g, m * P:(m + 1) * P], n2b[:, g:g + 1],
                           start=(m == 0 and g == 0), stop=(g == 1))
            s.then_inc(setup_pe, 1)
            pe.wait_ge(setup_v, V_BV)
            for e in range(2):
                s = mm(ps[0:1, 4, 0:C], bv[:, e:e + 1], wproj[:, e, :], start=(e == 0), stop=(e == 1))
            s.then_inc(setup_pe, 1)
            pe.wait_ge(setup_v, V_ALL)

            def x_transposes(t, par, post):
                pe.wait_ge(x_in[par], x_count(t, par))
                for n in range(4):
                    if n >= 2:
                        pe.wait_ge(xT_ready, signals(t, 4, n - 1))
                    elif post:
                        pe.wait_ge(h_ready, signals(t - 2, 2, n + 1))
                    elif not isinstance(t, int) or t > 0:
                        pe.wait_ge(k_lo_ready, signals(t, 4, n - 1))
                    g = n % 2
                    for k in range(4) if n < 2 else [4]:
                        s = pe.transpose(D[n % 2][:, (k % 4) * P:(k % 4 + 1) * P], xin[par][:, k, g * P:(g + 1) * P], ident[:])
                    s.then_inc(pe_x, 1)

            def q_product(t, par, post):
                pe.wait_ge(a_hi_ready, signals(t, G, G))
                pe.wait_ge(a_lo_ready, signals(t, G, G))
                for g in range(G):
                    if post:
                        pe.wait_ge(gelu_ready, signals(t - 2, MT, 2 + g + 1))
                    else:
                        pe.wait_ge(xT_ready, signals(t, 4, 2 + g + 1))
                    mm(D[g], bias[:, g * P:(g + 1) * P], ones16[:], start=True)
                    for kg in range(G):
                        ws = [w[:, kg, g * P:(g + 1) * P] for w in (wqkv_hi, wqkv_lo)]
                        tok = [a[par][:, kg].rearrange("p c (r j) -> p c r j", j=WIN)[:, :, 1:1 + TS, 1:1 + TS]
                               for a in (a_hi, a_lo)]
                        s = three(D[g], ws, tok, False, kg == G - 1)
                    s.then_inc(pe_q, 1)

            def k_product(t, par, g, half, bank):
                o = D[bank][:, 0:HALF]
                mm(o, bias[:, C + g * P:C + (g + 1) * P], ones16[:, 0:HALF], start=True)
                for kg in range(G):
                    ws = [w[:, kg, C + g * P:C + (g + 1) * P] for w in (wqkv_hi, wqkv_lo)]
                    tok = [keys(a[par], kg, half) for a in (a_hi, a_lo)]
                    s = three(o, ws, tok, False, kg == G - 1)
                s.then_inc(pe_k, 1)

            def projection(t, par):
                pe.wait_ge(o_hi_ready, signals(t, TILES, TILES))
                pe.wait_ge(o_lo_ready, signals(t, TILES, TILES))
                for g in range(G):
                    if isinstance(t, int) and t == BANDS - 1:
                        pe.wait_ge(y_ready, signals(t - 1, 2, g + 1))
                    else:
                        pe.wait_ge(k_lo_ready, signals(t + 1, 4, 2 + g + 1))
                    mm(D[g], bias[:, 2 * C + g * P:2 * C + (g + 1) * P], ones16[:], start=True)
                    for e in range(2):
                        s = three(D[g], [w[:, e, g * P:(g + 1) * P] for w in (wproj_hi, wproj_lo)],
                                  [o[par][:, e, :] for o in (o_hi, o_lo)], False, e == 1)
                    s.then_inc(pe_proj, 1)

            def mlp_in(t, pre):
                pe.wait_ge(b_hi_ready, signals(t, 1, 1))
                pe.wait_ge(b_lo_ready, signals(t, 1, 1))
                for m in range(MT):
                    if m >= 2:
                        pe.wait_ge(gelu_ready, signals(t, MT, m - 1))
                    elif pre:
                        pe.wait_ge(xT_ready, signals(t + 2, 4, 2 + m + 1))
                    else:
                        pe.wait_ge(h_ready, signals(t, 2, m + 1))
                    for g in range(G):
                        s = three(D[m % 2], [w[:, g, m * P:(m + 1) * P] for w in (w1_hi, w1_lo)],
                                  [b[:, g, :] for b in (b_hi, b_lo)], g == 0, g == G - 1)
                    s.then_inc(pe_m1, 1)

            def mlp_out(t, n, bank):
                for k in range(2):
                    tok = slice((2 * n + k) * P, (2 * n + k + 1) * P)
                    o = D[bank][:, k * C:(k + 1) * C]
                    mm(o, ones16[:, 0:P], bias[:, 3 * C:4 * C], start=(k == 0))
                    for m in range(MT):
                        if k == 0 and n == 0:
                            pe.wait_ge(g_lo_ready, signals(t, MT, m + 1))
                            pe.wait_ge(g_hi_ready, signals(t, MT, m + 1))
                        three(o, [g_[:, m, tok] for g_ in (g_hi, g_lo)], [w[:, m, :] for w in (w2_hi, w2_lo)],
                              False, False)
                    for g in range(G):
                        s = mm(o[:, g * P:(g + 1) * P], h[:, g, tok], ident_ws[:], stop=True)
                s.then_inc(pe_m2, 1)

            def scores(t, par, c):
                pe.wait_ge(maxrow_ready, signals(t, TILES, c))
                if c == 0:
                    pe.wait_ge(mask_in[par], mask_count(t, par))
                    pe.wait_ge(k_lo_ready, signals(t, 4, 4))
                    pe.wait_ge(q_lo_ready, signals(t, 2, 2))
                mm(ps[:, B_S, 0:PAIRS * NK], qmask[par][:, c, :], key_scores[:].rearrange("p a k -> p (a k)"), start=True)
                for p in range(PAIRS):
                    g = p // 2
                    s = mm(ps[:, B_S, p * NK:(p + 1) * NK],
                           q_hi[par][:, g, c, 2 * (p % 2):2 * (p % 2) + 2, :].rearrange("p h q -> p (h q)"),
                           window(k_hi[par], g, c), stop=True)
                s.then_inc(pe_s, 1)

            def values(t, par, c):
                pe.wait_ge(v_lo_ready, signals(t, TILES, c))
                if c == 0:
                    pe.wait_ge(a_lo_ready, signals(t, G, G))
                for g in range(G):
                    s = three(ps[0:NK, B_V, 0:C], [window(a[par], g, c) for a in (a_hi, a_lo)],
                              [w[:, g, 2 * C:3 * C] for w in (wqkv_hi, wqkv_lo)], g == 0, g == G - 1)
                s.then_inc(pe_v, 1)

            def scores_t(t, par, c):
                if exists(t, c - 2):
                    pe.wait_ge(p_hi_ready, signals(t, TILES, c - 1))
                for g in range(G):
                    o = ps[0:NK, B_ST + c % 2, g * 256:(g + 1) * 256]
                    three(o, [window(k[par], g, c) for k in (k_hi, k_lo)],
                          [q[par][:, g, c].rearrange("p h q -> p (h q)") for q in (q_hi, q_lo)], g == 0, False)

            def max_rows(t, c):
                pe.wait_ge(max_ready, signals(t, TILES, c + 1))
                pe.transpose(ps[:, B_S, PAIRS * NK:PAIRS * NK + P // 2].bitcast(F16), maxima[c % 2][:], ident16[:]).then_inc(pe_max, 1)

            def mask_t(t, par, c):
                pe.wait_ge(maxrow_ready, signals(t, TILES, c + 1))
                for p in range(PAIRS):
                    s = mm(ps[0:NK, B_ST + c % 2, p * P:(p + 1) * P], key_probs[:, p, :], qmask[par][:, c, :], stop=True)
                s.then_inc(pe_st, 1)

            def weighted(t, c):
                pe.wait_ge(p_lo_ready, signals(t, TILES, c + 1))
                pe.wait_ge(v_lo_ready, signals(t, TILES, c + 1))
                if exists(t, c - 1):
                    pe.wait_ge(norm_ready, signals(t, TILES, c))
                b = c % 2
                for p in range(PAIRS):
                    o = ps[:, B_AV, p * VW:(p + 1) * VW]
                    ph, pl = (q[b][0:NK, p * P:(p + 1) * P] for q in (p_hi, p_lo))
                    s = three(o, (ph, pl), (v_hi[b][0:NK, p, :], v_lo[b][0:NK, p, :]), p == 0, True)
                s.then_inc(pe_av, 1)

            def turn(t, c):
                pe.wait_ge(norm_ready, signals(t, TILES, c + 1))
                if exists(t, c - 1):
                    pe.wait_ge(o_lo_ready, signals(t, TILES, c))
                pe.transpose(ps[:, B_OT, 0:P], o_norm[c % 2][:].rearrange("p a d -> p (a d)"), ident[:]).then_inc(pe_ot, 1)

            def step(t, par, att, pre, post):
                new, old = 1 - par, 1 - par
                for c in range(TILES):
                    if att:
                        scores(t, par, c)
                        values(t, par, c)
                        scores_t(t, par, c)
                        max_rows(t, c)
                    if exists(t, c - 2):
                        turn(t, c - 2)
                    if c == 2 and post:
                        projection(t - 1, old)
                    if c == 2 and pre:
                        x_transposes(t + 1, new, post)
                    if c == 4 and post:
                        mlp_in(t - 1, pre)
                    if c == 5 and pre:
                        q_product(t + 1, new, post)
                    if c == 6:
                        if post:
                            pe.wait_ge(q_lo_ready, signals(t + 1, 2, 1)) if pre else pe.wait_ge(gelu_ready, signals(t - 1, MT, 3))
                            mlp_out(t - 1, 0, 0)
                        if pre:
                            pe.wait_ge(q_lo_ready, signals(t + 1, 2, 2))
                            k_product(t + 1, new, 0, 0, 1)
                            pe.wait_ge(y_ready, signals(t - 1, 2, 1)) if post else None
                            k_product(t + 1, new, 0, 1, 0)
                    if c == 7:
                        if post:
                            pe.wait_ge(k_lo_ready, signals(t + 1, 4, 1)) if pre else pe.wait_ge(gelu_ready, signals(t - 1, MT, 4))
                            mlp_out(t - 1, 1, 1)
                        if pre:
                            pe.wait_ge(k_lo_ready, signals(t + 1, 4, 2))
                            k_product(t + 1, new, 1, 0, 0)
                            pe.wait_ge(y_ready, signals(t - 1, 2, 2)) if post else pe.wait_ge(k_lo_ready, signals(t + 1, 4, 1))
                            k_product(t + 1, new, 1, 1, 1)
                    if att:
                        mask_t(t, par, c)
                    if exists(t, c - 1):
                        weighted(t, c - 1)

            run(pe, step)

        @block.vector
        def _(v):
            def zero(ap, value=0.0):
                v.memset(ap, value).then_inc(zeroed, 1)

            for t_ in (*q_hi, *q_lo):
                zero(t_[:].rearrange("p g c h q -> p (g c h q)").bitcast(U32), 0)
            for t_ in qmask:
                zero(t_[:].rearrange("p c q -> p (c q)").bitcast(U32), 0)
            for t_ in xT:
                zero(flat(t_))
            for t_ in maxima:
                zero(t_[:])
            for t_ in v_lo:
                zero(t_[:].rearrange("p a w -> p (a w)"))
            for t_ in v_hi:
                zero(t_[:].rearrange("p a w -> p (a w)"), 1.0)
            zero(bias[:])
            zero(ones16[:], 1.0)
            v.wait_ge(zeroed, N_ZERO)
            v.wait_ge(w_in, 16 * N_LOADS)

            count = [0]

            def link(ins):
                count[0] += 1
                ins.then_inc(setup_v, 1)
                v.wait_ge(setup_v, count[0])

            v.wait_ge(setup_pe, 1)
            link(v.tensor_tensor(bv[:], bv_in[:], ps[:, 1:3, 0], ALU.add))
            assert count[0] == V_BV
            link(v.tensor_tensor(b1[:], b1_in[:], ps[:, 3, 0:MT], ALU.add))

            def split(hi, lo, src, parts, n):
                for cols, rowf, f in parts:
                    d = wscaled[:, cols]
                    if rowf is None:
                        link(v.tensor_scalar(d, src[:, cols], f, None, ALU.mult))
                    else:
                        link(v.tensor_scalar(d, src[:, cols], rowf, f, ALU.mult, ALU.mult))
                link(v.tensor_copy(hi, wscaled[:, 0:n]))
                link(v.tensor_tensor(lo, wscaled[:, 0:n], hi, ALU.subtract))

            parts = []
            for g in range(G):
                a = g * 3 * C
                parts.append((slice(a, a + C), n1w[:, g:g + 1], WS * HD ** -0.5))
                parts.append((slice(a + C, a + 3 * C), n1w[:, g:g + 1], WS))
            split(flat2(wqkv_hi), flat2(wqkv_lo), flat2(wqkv), parts, G * 3 * C)
            split(flat2(wproj_hi), flat2(wproj_lo), flat2(wproj), [(slice(0, 2 * C), None, WS)], 2 * C)
            split(flat2(w1_hi), flat2(w1_lo), flat2(w1),
                  [(slice(g * HID, (g + 1) * HID), n2w[:, g:g + 1], WS) for g in range(G)], G * HID)
            split(flat2(w2_hi), flat2(w2_lo), flat2(w2), [(slice(0, MT * C), None, WS)], MT * C)
            link(v.tensor_tensor(brow[:, 0:2 * C], brow_in[:, 0:2 * C], ps[0:1, 0, :], ALU.add))
            v.wait_ge(setup_pe, 2)
            link(v.tensor_tensor(brow[:, 2 * C:3 * C], brow_in[:, 2 * C:3 * C], ps[0:1, 4, 0:C], ALU.add))
            link(v.tensor_scalar(brow[:, C:3 * C], brow[:, C:3 * C], WS, None, ALU.mult))
            link(v.tensor_scalar(brow[:, 0:C], brow[:, 0:C], WS * HD ** -0.5, None, ALU.mult))
            link(v.tensor_scalar(brow[:, 3 * C:4 * C], brow_in[:, 3 * C:4 * C], WS, None, ALU.mult))
            link(v.tensor_copy(bias[0:1, :], brow[:, :]))
            link(v.tensor_tensor(brow[:, :], brow[:, :], bias[0:1, :], ALU.subtract))
            link(v.tensor_copy(brow16, brow))
            link(v.tensor_copy(bias[32:33, :], brow16))
            link(v.tensor_tensor(brow, brow, brow16, ALU.subtract))
            link(v.tensor_copy(bias[64:65, :], brow[:, :]))
            assert count[0] == V_ALL, count[0]

            def h_from_projection(t, par):
                v.wait_ge(pe_m2, signals(t, 2, 0))
                for g in range(G):
                    v.wait_ge(pe_proj, signals(t, 2, g + 1))
                    v.scalar_tensor_tensor(
                        out=h[:, g, :].rearrange("p (i j) -> p i j", j=SIDE),
                        in0=ps[:, g, :].rearrange("p (i j) -> p i j", j=SIDE), scalar=INV,
                        in1=xT[par][:, g, 1:1 + TS, 1:1 + SIDE], op0=ALU.mult, op1=ALU.add).then_inc(h_ready, 1)

            def magnitude(out, of, s):
                v.tensor_single_scalar(out.bitcast(U32), of.bitcast(U32), MAGNITUDE, ALU.bitwise_and).then_inc(s, 1)

            def with_sign(out, sign_of, log, s):
                v.scalar_tensor_tensor(out=out.bitcast(U32), in0=sign_of.bitcast(U32), scalar=SIGN, in1=log.bitcast(U32),
                                       op0=ALU.bitwise_and, op1=ALU.bitwise_or).then_inc(s, 1)

            def x_from_transposes(t, par):
                for n in range(4):
                    v.wait_ge(pe_x, signals(t, 4, n + 1))
                    rows = slice(0, TS) if n < 2 else slice(TS, XROWS)
                    size = (rows.stop - rows.start) * SIDE
                    v.tensor_copy(xT[par][:, n % 2, rows, 1:1 + SIDE],
                                  ps[:, n % 2, 0:size].rearrange("p (i j) -> p i j", j=SIDE)).then_inc(xT_ready, 1)

            def q_low(t, par):
                for g in range(G):
                    v.wait_ge(q_hi_ready, signals(t, 2, g + 1))
                    for n in range(4):
                        r = slice(HD * n, HD * n + HD)
                        s = v.scalar_tensor_tensor(
                            out=q_lo[par][r, g, :, n, :], in0=ps[r, g, :].rearrange("p (c q) -> p c q", q=NQ), scalar=INV,
                            in1=q_hi[par][r, g, :, n, :], op0=ALU.mult, op1=ALU.subtract)
                    s.then_inc(q_lo_ready, 1)

            def k_low(t, par, g, half, bank):
                v.wait_ge(k_hi_ready, signals(t, 4, 2 * g + half + 1))
                v.scalar_tensor_tensor(
                    out=keys(k_lo[par], g, half), in0=ps[:, bank, 0:HALF], scalar=INV, in1=keys(k_hi[par], g, half),
                    op0=ALU.mult, op1=ALU.subtract).then_inc(k_lo_ready, 1)

            def tile_maximum(t, c):
                v.wait_ge(pe_s, signals(t, TILES, c + 1))
                v.tensor_reduce(maxima[c % 2][:, M0:M0 + PAIRS], ps[:, B_S, 0:PAIRS * NK].rearrange("p (a k) -> p a k", k=NK),
                                AX.X, ALU.max).then_inc(max_ready, 1)

            def v_low(t, c):
                v.wait_ge(v_hi_ready, signals(t, TILES, c + 1))
                b = c % 2
                v.scalar_tensor_tensor(
                    out=v_lo[b][0:NK, :, 0:2 * HD], in0=ps[0:NK, B_V, 0:C].rearrange("p (a d) -> p a d", d=2 * HD),
                    scalar=INV, in1=v_hi[b][0:NK, :, 0:2 * HD], op0=ALU.mult, op1=ALU.subtract).then_inc(v_lo_ready, 1)

            def maxima_to_mask(t, par, c):
                v.wait_ge(pe_max, signals(t, TILES, c + 1))
                v.tensor_copy(qmask[par][M0:M0 + PAIRS, c, :],
                              ps[M0:M0 + PAIRS, B_S, PAIRS * NK:PAIRS * NK + P // 2].bitcast(F16)).then_inc(maxrow_ready, 1)

            def o_low(t, par, c):
                v.wait_ge(o_hi_ready, signals(t, TILES, c + 1))
                v.tensor_tensor(o_tile(o_lo[par], c), ps_ot(), o_tile(o_hi[par], c), ALU.subtract).then_inc(o_lo_ready, 1)

            def normalise(t, c):
                b = c % 2
                av = ps[:, B_AV, 0:PAIRS * VW].rearrange("p (a w) -> p a w", w=VW)
                v.wait_ge(pe_av, signals(t, TILES, c + 1))
                v.reciprocal(recip[b][:], av[:, :, 2 * HD:VW]).then_inc(recip_ready, 1)
                v.wait_ge(recip_ready, signals(t, TILES, c + 1))
                for e in range(2):
                    r = slice(NQ * e, NQ * e + NQ)
                    s = v.tensor_tensor(o_norm[b][r], av[r, :, HD * e:HD * e + HD],
                                        recip[b][r].to_broadcast([NQ, PAIRS, HD]), ALU.mult)
                s.then_inc(norm_ready, 1)

            def step(t, par, att, pre, post):
                new = old = 1 - par
                for c in range(TILES):
                    if att:
                        tile_maximum(t, c)
                        v_low(t, c)
                        maxima_to_mask(t, par, c)
                    if exists(t, c - 2):
                        o_low(t, par if c >= 2 else old, c - 2)
                    if c == 2 and post:
                        h_from_projection(t - 1, old)
                        v.wait_ge(h_ready, signals(t - 1, 2, 2))
                        v.wait_ge(b_lo_ready, signals(t - 1, 1, 0))
                        magnitude(ln2_u[:], flat2(h), abs2)
                    if c == 2 and pre:
                        x_from_transposes(t + 1, new)
                    if c == 3 and pre:
                        v.wait_ge(xT_ready, signals(t + 1, 4, 4))
                        v.wait_ge(a_lo_ready, signals(t + 1, G, 0))
                        magnitude(ln1_u[:], flat(xT[new]), abs1)
                    if c == 3 and post:
                        v.wait_ge(abs2, signals(t - 1, 1, 1))
                        v.wait_ge(root2, signals(t - 1, 1, 1))
                        v.tensor_tensor(ln2_u[:], ln2_u[:], ln2_s[:], ALU.add).then_inc(sum2, 1)
                        v.wait_ge(log2, signals(t - 1, 1, 1))
                        with_sign(ln2_u[:], flat2(h), ln2_s[:], asinh2)
                        v.wait_ge(asinh2, signals(t - 1, 1, 1))
                        v.wait_ge(pe_m1, signals(t - 1, MT, 0))
                        v.tensor_copy(flat2(b_hi), ln2_u[:]).then_inc(b_hi_ready, 1)
                    if c == 4 and pre:
                        v.wait_ge(abs1, signals(t + 1, 1, 1))
                        v.wait_ge(root1, signals(t + 1, 1, 1))
                        v.tensor_tensor(ln1_u[:], ln1_u[:], ln1_s[:], ALU.add).then_inc(sum1, 1)
                        v.wait_ge(log1, signals(t + 1, 1, 1))
                        with_sign(ln1_u[:], flat(xT[new]), ln1_s[:], asinh1)
                        v.wait_ge(asinh1, signals(t + 1, 1, 1))
                        for g in range(G):
                            v.tensor_copy(by_window(a_hi[new], g), in_windows(ln1_u, g)).then_inc(a_hi_ready, 1)
                    if c == 4 and post:
                        for m in range(MT):
                            v.wait_ge(gelu_ready, signals(t - 1, MT, m + 1))
                            v.tensor_copy(g_hi[:, m, :], g32[:, m, :]).then_inc(g_hi_ready, 1)
                    if c == 5 and pre:
                        q_low(t + 1, new)
                    if c >= 6 and pre:
                        k_low(t + 1, new, c - 6, 0, 1 if c == 6 else 0)
                        k_low(t + 1, new, c - 6, 1, 0 if c == 6 else 1)
                    if exists(t, c - 1):
                        normalise(t, c - 1)

            run(v, step)

        @block.scalar
        def _(act):
            act.wait_ge(zeroed, N_ZERO)
            act.wait_ge(setup_v, V_ALL)

            log_exp_set, gelu_set = "natural_log_exp_and_others", "gelu_and_others"
            act.preload_act_table_set(log_exp_set)

            def root(s, of, done):
                (sq, n_sq), (ln, n_ln), (rt, n_rt) = done
                act.activation(s, of, ACT.Square).then_inc(sq, 1)
                act.wait_ge(sq, signals(n_sq, 1, 1))
                act.activation(s, s, ACT.Ln, bias=1.0).then_inc(ln, 1)
                act.wait_ge(ln, signals(n_ln, 1, 1))
                act.activation(s, s, ACT.Exp, scale=0.5).then_inc(rt, 1)

            def q_high(t, par):
                for g in range(G):
                    act.wait_ge(pe_q, signals(t, 2, g + 1))
                    for n in range(4):
                        r = slice(HD * n, HD * n + HD)
                        s = act.activation(q_hi[par][r, g, :, n, :], ps[r, g, :].rearrange("p (c q) -> p c q", q=NQ),
                                           ACT.Copy, scale=INV)
                    s.then_inc(q_hi_ready, 1)

            def k_high(t, par, g, half, bank):
                act.wait_ge(pe_k, signals(t, 4, 2 * g + half + 1))
                act.activation(keys(k_hi[par], g, half), ps[:, bank, 0:HALF], ACT.Copy, scale=INV).then_inc(k_hi_ready, 1)

            def result(t, n):
                act.wait_ge(pe_m2, signals(t, 2, n + 1))
                act.wait_ge(y_out[n], signals(t, 16, 0))
                act.activation(flat2(y[n]), ps[:, n, :], ACT.Copy, scale=INV).then_inc(y_ready, 1)

            def v_high(t, c):
                act.wait_ge(pe_v, signals(t, TILES, c + 1))
                if exists(t, c - 2):
                    act.wait_ge(pe_av, signals(t, TILES, c - 1))
                act.activation(v_hi[c % 2][0:NK, :, 0:2 * HD], ps[0:NK, B_V, 0:C].rearrange("p (a d) -> p a d", d=2 * HD),
                               ACT.Copy, scale=INV).then_inc(v_hi_ready, 1)

            def o_high(t, par, c):
                act.wait_ge(pe_ot, signals(t, TILES, c + 1))
                if c == 0:
                    act.wait_ge(pe_proj, signals(t - 1, 2, 0))
                act.activation(o_tile(o_hi[par], c), ps_ot(), ACT.Copy).then_inc(o_hi_ready, 1)

            def probabilities(t, c):
                b = c % 2
                act.wait_ge(pe_st, signals(t, TILES, c + 1))
                if exists(t, c - 2):
                    act.wait_ge(p_lo_ready, signals(t, TILES, c - 1))
                act.activation(prob[b][0:NK], ps[0:NK, B_ST + b, :], ACT.Exp).then_inc(prob_ready, 1)
                act.activation(p_hi[b][0:NK], ps[0:NK, B_ST + b, :], ACT.Exp).then_inc(p_hi_ready, 1)

            def step(t, par, att, pre, post):
                new = old = 1 - par
                for c in range(TILES):
                    if att:
                        v_high(t, c)
                    if exists(t, c - 2):
                        o_high(t, par if c >= 2 else old, c - 2)
                    if c == 2 and post:
                        act.wait_ge(h_ready, signals(t - 1, 2, 2))
                        act.wait_ge(asinh2, signals(t - 1, 1, 0))
                        root(ln2_s[:], flat2(h), [(sq2, t - 1), (ln2a, t - 1), (root2, t - 1)])
                    if c == 3 and post:
                        act.wait_ge(sum2, signals(t - 1, 1, 1))
                        act.activation(ln2_s[:], ln2_u[:], ACT.Ln).then_inc(log2, 1)
                    if c == 3 and pre:
                        act.wait_ge(xT_ready, signals(t + 1, 4, 4))
                        act.wait_ge(asinh1, signals(t + 1, 1, 0))
                        root(ln1_s[:], flat(xT[new]), [(sq1, t + 1), (ln1a, t + 1), (root1, t + 1)])
                    if c == 4 and pre:
                        act.wait_ge(sum1, signals(t + 1, 1, 1))
                        act.activation(ln1_s[:], ln1_u[:], ACT.Ln).then_inc(log1, 1)
                    if c == 4 and post:
                        act.preload_act_table_set(gelu_set)
                        act.wait_ge(g_lo_ready, signals(t - 1, MT, 0))
                        for m in range(MT):
                            act.wait_ge(pe_m1, signals(t - 1, MT, m + 1))
                            act.activation(g32[:, m, :], ps[:, m % 2, :], ACT.Gelu, bias=b1[:, m:m + 1],
                                           scale=INV).then_inc(gelu_ready, 1)
                        act.preload_act_table_set(log_exp_set)
                    if c == 5 and pre:
                        q_high(t + 1, new)
                    if c >= 6 and post:
                        result(t - 1, c - 6)
                    if c >= 6 and pre:
                        k_high(t + 1, new, c - 6, 0, 1 if c == 6 else 0)
                        k_high(t + 1, new, c - 6, 1, 0 if c == 6 else 1)
                    if att:
                        probabilities(t, c)

            run(act, step)

        @block.gpsimd
        def _(pool):
            def step(t, par, att, pre, post):
                new = 1 - par
                for c in range(TILES):
                    if c == 3 and post:
                        pool.wait_ge(b_hi_ready, signals(t - 1, 1, 1))
                        pool.tensor_tensor(flat2(b_lo), ln2_u[:], flat2(b_hi), ALU.subtract).then_inc(b_lo_ready, 1)
                    if c == 4 and pre:
                        for g in range(G):
                            pool.wait_ge(a_hi_ready, signals(t + 1, G, g + 1))
                            pool.tensor_tensor(by_window(a_lo[new], g), in_windows(ln1_u, g), by_window(a_hi[new], g),
                                               ALU.subtract).then_inc(a_lo_ready, 1)
                    if c == 4 and post:
                        for m in range(MT):
                            pool.wait_ge(g_hi_ready, signals(t - 1, MT, m + 1))
                            pool.tensor_tensor(g_lo[:, m, :], g32[:, m, :], g_hi[:, m, :], ALU.subtract).then_inc(g_lo_ready, 1)
                    if att:
                        pool.wait_ge(p_hi_ready, signals(t, TILES, c + 1))
                        if exists(t, c - 2):
                            pool.wait_ge(pe_av, signals(t, TILES, c - 1))
                        b = c % 2
                        pool.tensor_tensor(p_lo[b][0:NK], prob[b][0:NK], p_hi[b][0:NK], ALU.subtract).then_inc(p_lo_ready, 1)

            run(pool, step)


_INS = ["x", "qkv_w", "qkv_b", "proj_w", "proj_b", "n1_w", "n1_b", "n2_w", "n2_b", "mlp_w1", "mlp_b1", "mlp_w2", "mlp_b2"]


def kernel(**inputs):
    import concourse.bacc as _bacc
    from concourse.bass_utils import run_bass_kernel_spmd as _run

    nc = _bacc.Bacc("TRN2", target_bir_lowering=False, num_devices=1)
    arrays, args = {}, []
    given = [(n, np.ascontiguousarray(inputs[n if n == "x" else "L0_conv_" + n])) for n in _INS]
    for name, a in given + list(constants().items()):
        arrays[f"in_{name}_dram"] = a
        args.append(nc.dram_tensor(f"in_{name}_dram", a.shape, mybir.dt.from_np(a.dtype), kind="ExternalInput").ap())
    args.append(nc.dram_tensor("out_dram", (IMAGES, SIDE, SIDE, C), F32, kind="ExternalOutput").ap())
    build(nc, *args)
    r = _run(nc, [arrays], core_ids=[0])
    return r.results[0]["out_dram"]
```

```python
from contextlib import ExitStack

import numpy as np

import concourse.bass as bass
from concourse import mybir

ALU = mybir.AluOpType
ACT = mybir.ActivationFunctionType
F32 = mybir.dt.float32
F16 = mybir.dt.float16
BF16 = mybir.dt.bfloat16
U32 = mybir.dt.uint32
AX = mybir.AxisListType

P = 128
IMAGES, SIDE, C = 16, 64, 256
HEADS = 8
HD = C // HEADS
HID = 2 * C
G = C // P
PAIRS = HEADS // 2
TS = 8
WIN = TS + 2
NK = WIN * WIN
NQ = TS * TS
TILES = SIDE // TS
BPI = SIDE // TS
BANDS = IMAGES * BPI
TOK = TS * SIDE
XROWS = WIN
XTOK = XROWS * SIDE
PITCH = SIDE + 2
PADTOK = XROWS * PITCH
HALF = TILES // 2 * NK
VW = 2 * HD + 1
MT = HID // P
WS = 16.0
INV = 1.0 / WS
M0 = 32
MASKED_Q, MASKED_K = -32768.0, 32768.0
KPAD = P - NK
SIGN, MAGNITUDE = 0x80000000, 0x7FFFFFFF

N_LOADS = 16 + 2 * PAIRS
N_ZERO = 24
V_BV, V_ALL = 1, 30

B_S, B_ST, B_V, B_AV = 3, 4, 6, 7
OT_COLS = slice(3 * P, 4 * P)
P_BANK = [1, 2]
X_BANK = [0, 1, 2, 0]
OUT_BANK = [0, 1]
IN_BANK = [2, 0, 1, 2]
Q_BANK = [0, 1]
K_PARTS = [(0, 0), (1, 0), (0, 1), (1, 1)]
K_BANK = [2, 0, 1, 2]


def bfloat16_bits(a):
    return (np.ascontiguousarray(a, np.float32).view(np.uint32) >> 16).astype(np.uint16)


def constants():
    ident = np.eye(P, dtype=np.float32)
    ident_ws = np.eye(P, dtype=np.float32) * np.float32(WS)
    marks = np.zeros((P, WIN, WIN), np.float32)
    for r in range(WIN):
        marks[r, r, :] = MASKED_K
        marks[WIN + r, :, r] = MASKED_K
    marks = marks.reshape(P, 1, NK)
    key_scores = np.repeat(marks, PAIRS, axis=1)
    key_probs = np.concatenate([key_scores, np.zeros((P, PAIRS, KPAD), np.float32)], axis=2)
    for p in range(PAIRS):
        key_probs[[M0 + p, M0 + PAIRS + p], p, :NK] = -1.0
    query = np.zeros((BPI, 2 * WIN, TILES, 2, TS, TS), np.float32)
    for b in range(BPI):
        for q in range(TS):
            first = min(max(TS * b + q - 1, 0), SIDE - 3)
            for r in range(WIN):
                if not first <= TS * b - 1 + r < first + 3:
                    query[b, r, :, :, q, :] = MASKED_Q
    for c in range(TILES):
        for q in range(TS):
            first = min(max(TS * c + q - 1, 0), SIDE - 3)
            for r in range(WIN):
                if not first <= TS * c - 1 + r < first + 3:
                    query[:, WIN + r, c, :, :, q] = MASKED_Q
    return {
        "ident": ident,
        "ident_ws": ident_ws,
        "ident16": bfloat16_bits(np.eye(P)),
        "key_scores": bfloat16_bits(key_scores.reshape(P, PAIRS * NK)),
        "key_probs": bfloat16_bits(key_probs.reshape(P, PAIRS * P)),
        "query_mask": bfloat16_bits(query.reshape(BPI, 2 * WIN, TILES * P)),
    }


def build(nc, x, qkv_w, qkv_b, proj_w, proj_b, n1_w, n1_b, n2_w, n2_b, mlp_w1, mlp_b1, mlp_w2, mlp_b2,
          ident_c, ident_ws_c, ident16_c, key_scores_c, key_probs_c, query_mask_c, out):
    x_rows = x.rearrange("i r j c -> (i r j) c")
    out_rows = out.rearrange("i r j c -> (i r j) c")

    with ExitStack() as ctx:
        def sb(name, shape, dt):
            return ctx.enter_context(nc.sbuf_tensor(name, shape, dt))

        def sem(name):
            return ctx.enter_context(nc.semaphore(name))

        ps = ctx.enter_context(nc.psum_tensor("ps", [P, 8, 512], F32))

        ident = sb("ident", [P, P], F32)
        ident_ws = sb("ident_ws", [P, P], F32)
        ident16 = sb("ident16", [P, P], BF16)
        key_scores = sb("key_scores", [P, PAIRS, NK], BF16)
        key_probs = sb("key_probs", [P, PAIRS, P], BF16)
        ones16 = sb("ones16", [P, TOK], F16)
        wqkv = sb("wqkv", [P, G, 3 * C], F32)
        wproj = sb("wproj", [P, 2, C], F32)
        w1 = sb("w1", [P, G, HID], F32)
        w2 = sb("w2", [P, MT, C], F32)
        wqkv_hi, wqkv_lo = sb("wqkv_hi", [P, G, 3 * C], F16), sb("wqkv_lo", [P, G, 3 * C], F16)
        wproj_hi, wproj_lo = sb("wproj_hi", [P, 2, C], F16), sb("wproj_lo", [P, 2, C], F16)
        w1_hi, w1_lo = sb("w1_hi", [P, G, HID], F16), sb("w1_lo", [P, G, HID], F16)
        w2_hi, w2_lo = sb("w2_hi", [P, MT, C], F16), sb("w2_lo", [P, MT, C], F16)
        n1w, n1b = sb("n1w", [P, G], F32), sb("n1b", [P, G], F32)
        n2w, n2b = sb("n2w", [P, G], F32), sb("n2b", [P, G], F32)
        bv_in, bv = sb("bv_in", [P, 2], F32), sb("bv", [P, 2], F32)
        b1_in, b1 = sb("b1_in", [P, MT], F32), sb("b1", [P, MT], F32)
        bqk_in, bqk = sb("bqk_in", [P, 2 * G], F32), sb("bqk", [P, 2 * G], F32)
        bias = sb("bias", [P, 2 * C], F16)

        xin = [sb(f"xin{i}", [P, XTOK // P, C], F32) for i in range(2)]
        xT = [sb(f"xT{i}", [P, G, XROWS, PITCH], F32) for i in range(2)]
        a_hi = [sb(f"a_hi{i}", [P, G, TILES * NK + KPAD], F16) for i in range(2)]
        a_lo = [sb(f"a_lo{i}", [P, G, TILES * NK + KPAD], F16) for i in range(2)]
        k_hi = [sb(f"k_hi{i}", [P, G, TILES * NK + KPAD], F16) for i in range(2)]
        k_lo = [sb(f"k_lo{i}", [P, G, TILES * NK + KPAD], F16) for i in range(2)]
        q_hi = [sb(f"q_hi{i}", [P, G, TILES, 4, NQ], F16) for i in range(2)]
        q_lo = [sb(f"q_lo{i}", [P, G, TILES, 4, NQ], F16) for i in range(2)]
        qmask = [sb(f"qmask{i}", [P, TILES, P], BF16) for i in range(2)]
        o_hi = [sb(f"o_hi{i}", [P, 2, TOK], F16) for i in range(2)]
        o_lo = [sb(f"o_lo{i}", [P, 2, TOK], F16) for i in range(2)]
        v_hi = [sb(f"v_hi{i}", [P, PAIRS, VW], F16) for i in range(2)]
        v_lo = [sb(f"v_lo{i}", [P, PAIRS, VW], F16) for i in range(2)]
        prob = [sb(f"prob{i}", [P, 512], F32) for i in range(2)]
        p_hi = [sb(f"p_hi{i}", [P, 512], F16) for i in range(2)]
        p_lo = [sb(f"p_lo{i}", [P, 512], F16) for i in range(2)]
        max32 = [sb(f"max32{i}", [P, PAIRS], F32) for i in range(2)]
        maxima = [sb(f"maxima{i}", [P, P], BF16) for i in range(2)]
        recip = [sb(f"recip{i}", [P, PAIRS, 1], F32) for i in range(2)]
        o_norm = [sb(f"o_norm{i}", [P, PAIRS, HD], F32) for i in range(2)]
        ln1_s, ln1_u = sb("ln1_s", [P, G * PADTOK], F32), sb("ln1_u", [P, G * PADTOK], F32)
        ln2_s, ln2_u = sb("ln2_s", [P, G * TOK], F32), sb("ln2_u", [P, G * TOK], F32)
        h = [sb(f"h{i}", [P, G, TOK], F32) for i in range(2)]
        b_hi, b_lo = sb("b_hi", [P, G, TOK], F16), sb("b_lo", [P, G, TOK], F16)
        g32 = sb("g32", [P, MT, TOK], F32)
        g_hi, g_lo = sb("g_hi", [P, MT, TOK], F16), sb("g_lo", [P, MT, TOK], F16)
        y = [sb(f"y{i}", [P, 2, C], F32) for i in range(2)]
        wscaled = sb("wscaled", [P, G * 3 * C], F32)
        brow_in = g32[0:1, 0, :]
        brow = g32[0:1, 1, :]
        brow16 = g_hi[0:1, 0, :]

        w_in = sem("w_in")
        x_in = [sem("x_in0"), sem("x_in1")]
        edge_in = sem("edge_in")
        mask_in = [sem("mask_in0"), sem("mask_in1")]
        y_out = [sem("y_out0"), sem("y_out1")]
        zeroed, setup_v, setup_pe = sem("zeroed"), sem("setup_v"), sem("setup_pe")
        pe_x, pe_q, pe_k, pe_proj, pe_m1, pe_m2 = (sem("pe_" + s) for s in ("x", "q", "k", "proj", "m1", "m2"))
        pe_s, pe_v, pe_max, pe_st, pe_av, pe_ot = (sem("pe_" + s) for s in ("s", "v", "max", "st", "av", "ot"))
        xT_ready, h_ready, abs1, abs2, sum1, sum2 = (sem("dve_" + s) for s in ("xT", "h", "abs1", "abs2", "sum1", "sum2"))
        asinh1, asinh2, a_hi_ready, b_hi_ready = (sem("dve_" + s) for s in ("asinh1", "asinh2", "a_hi", "b_hi"))
        q_lo_ready, k_lo_ready, g_hi_ready = (sem("dve_" + s) for s in ("q_lo", "k_lo", "g_hi"))
        max32_ready, max_hi_ready, max_ready = (sem("dve_" + s) for s in ("max32", "max_hi", "max"))
        v_lo_ready, maxrow_ready = sem("dve_v_lo"), sem("dve_maxrow")
        recip_ready, norm_ready, o_lo_ready = (sem("dve_" + s) for s in ("recip", "norm", "o_lo"))
        sq1, ln1a, root1, log1, sq2, ln2a, root2, log2 = (
            sem("act_" + s) for s in ("sq1", "ln1a", "root1", "log1", "sq2", "ln2a", "root2", "log2"))
        q_hi_ready, k_hi_ready, gelu_ready, y_ready = (sem("act_" + s) for s in ("q_hi", "k_hi", "gelu", "y"))
        v_hi_ready, prob_ready, p_hi_ready, o_hi_ready = (sem("act_" + s) for s in ("v_hi", "prob", "p_hi", "o_hi"))
        a_lo_ready, b_lo_ready, g_lo_ready, p_lo_ready = (sem("pool_" + s) for s in ("a_lo", "b_lo", "g_lo", "p_lo"))

        block = ctx.enter_context(nc.Block())

        def flat(t):
            return t[:].rearrange("p g r c -> p (g r c)")

        def flat2(t):
            return t[:].rearrange("p g n -> p (g n)")

        def o_tile(o, c):
            return o[:].rearrange("p e (i c j) -> p e c i j", c=TILES, j=TS)[:, :, c % TILES]

        def ps_ot():
            return ps[:, B_AV, OT_COLS].rearrange("p (e i j) -> p e i j", e=2, j=TS)

        def exists(t, c):
            return not isinstance(t, int) or 0 <= TILES * t + c < TILES * BANDS

        def signals(t, per, n):
            return max(t * per + n, 0) if isinstance(t, int) else t * per + n

        def run(eng, step):
            step(-1, 1, False, True, False, False)
            step(0, 0, True, True, False, False)
            step(1, 1, True, True, True, False)
            with eng.Fori(0, (BANDS - 4) // 2) as i:
                step(i * 2 + 2, 0, True, True, True, True)
                step(i * 2 + 3, 1, True, True, True, True)
            step(BANDS - 2, 0, True, True, True, True)
            step(BANDS - 1, 1, True, False, True, True)
            step(BANDS, 0, False, False, True, True)
            step(BANDS + 1, 1, False, False, False, True)

        def window(t, g, c):
            return t[:, g, NK * c:NK * c + P]

        def keys(t, g, half):
            return t[:, g, half * HALF:(half + 1) * HALF]

        def by_window(t, g):
            return t[:, g, 0:TILES * NK].rearrange("p (c r j) -> p c r j", r=WIN, j=WIN)

        def in_windows(u, g):
            a = u[:, g * PADTOK:(g + 1) * PADTOK]
            return bass.AP(a.tensor, a.offset, [list(a.ap[0]), [TS, TILES], [PITCH, WIN], [1, WIN]])

        @block.sync
        def _(sp):
            loads = [
                (ident[:], ident_c), (ident_ws[:], ident_ws_c), (ident16[:], ident16_c.bitcast(BF16)),
                (key_scores[:].rearrange("p a k -> p (a k)"), key_scores_c.bitcast(BF16)),
                (key_probs[:].rearrange("p a k -> p (a k)"), key_probs_c.bitcast(BF16)),
                (wqkv[:], qkv_w.rearrange("(g p) n -> p g n", p=P)),
                (w1[:], mlp_w1.rearrange("(g p) n -> p g n", p=P)),
                (w2[:], mlp_w2.rearrange("(m p) n -> p m n", p=P)),
                (n1w[:], n1_w.rearrange("(g p) -> p g", p=P)), (n1b[:], n1_b.rearrange("(g p) -> p g", p=P)),
                (n2w[:], n2_w.rearrange("(g p) -> p g", p=P)), (n2b[:], n2_b.rearrange("(g p) -> p g", p=P)),
                (b1_in[:], mlp_b1.rearrange("(m p) -> p m", p=P)),
                (bqk_in[:], qkv_b[0:2 * C].rearrange("(n p) -> p n", p=P)),
                (brow_in[:, 0:C], proj_b.rearrange("(a n) -> a n", a=1)),
                (brow_in[:, C:2 * C], mlp_b2.rearrange("(a n) -> a n", a=1)),
            ]
            wp = proj_w.rearrange("(p e d) n -> p d e n", p=PAIRS, e=2)
            bvp = qkv_b[2 * C:3 * C].rearrange("(p e d) -> p d e", p=PAIRS, e=2)
            for p in range(PAIRS):
                loads.append((wproj[HD * p:HD * p + HD], wp[p]))
                loads.append((bv_in[HD * p:HD * p + HD], bvp[p]))
            assert len(loads) == N_LOADS
            for to, of in loads:
                sp.dma_start(to, of, allow_slow_non_contiguous=True).then_inc(w_in, 16)

            def load_x(t, par):
                sp.dma_start(xin[par][:], x_rows[bass.ds(t * TOK - SIDE, XTOK)].rearrange("(k p) c -> p k c", p=P)
                             ).then_inc(x_in[par], 16)

            def load_edge_x(t, par):
                above = t == 0
                beyond = 0 if above else XROWS - 1
                tiles = slice(1, XTOK // P) if above else slice(0, XTOK // P - 1)
                beside = 1 if above else XROWS - 2
                edge = t * TOK if above else (t + 1) * TOK - SIDE
                for slot in (beyond, beside):
                    at = slot * SIDE
                    sp.dma_start(xin[par][at % P:at % P + SIDE, at // P, :], x_rows[edge:edge + SIDE]).then_inc(edge_in, 16)
                sp.wait_ge(edge_in, 32 if above else 64)
                first = t * TOK - SIDE + tiles.start * P
                sp.dma_start(xin[par][:, tiles, :], x_rows[first:first + 4 * P].rearrange("(k p) c -> p k c", p=P)
                             ).then_inc(x_in[par], 16)

            def load_mask(t, par, b):
                sp.dma_start(qmask[par][0:2 * WIN].rearrange("k c q -> k (c q)"), query_mask_c[b].bitcast(BF16)).then_inc(mask_in[par], 16)

            def store_y(t, par):
                for n in range(2):
                    sp.wait_ge(y_ready, signals(t, 2, n + 1))
                    dst = out_rows[bass.ds(t * TOK + n * 2 * P, 2 * P)]
                    sp.dma_start(dst.rearrange("(k p) c -> p k c", p=P), y[n][:]).then_inc(y_out[n], 16)

            sp.wait_ge(zeroed, N_ZERO)
            load_edge_x(0, 0)
            load_mask(0, 0, 0)
            load_x(1, 1)
            load_mask(1, 1, 1)

            def step(t, par, stores=True):
                sp.wait_ge(pe_x, signals(t, 4, 0))
                load_x(t + 1, 1 - par)
                sp.wait_ge(pe_st, signals(t, TILES, 0))
                load_mask(t + 1, 1 - par, (t + 1) % BPI)
                if stores:
                    store_y(t - 2, par)

            step(1, 1, False)
            with sp.Fori(0, (BANDS - 4) // 2) as i:
                step(i * 2 + 2, 0)
                step(i * 2 + 3, 1)
            sp.wait_ge(pe_x, signals(BANDS - 2, 4, 0))
            load_edge_x(BANDS - 1, 1)
            sp.wait_ge(pe_st, signals(BANDS - 2, TILES, 0))
            load_mask(BANDS - 1, 1, BPI - 1)
            for t in range(BANDS - 4, BANDS):
                store_y(t, t % 2)
            for n in range(2):
                sp.wait_ge(y_out[n], 16 * BANDS)

        def x_count(t, par):
            return (t // 2) * 16 + 16

        def mask_count(t, par):
            return (t // 2) * 16 + 16

        @block.tensor
        def _(pe):
            D = [ps[:, n, :] for n in range(3)]

            def mm(o, a, b, start=False, stop=False):
                return pe.matmul(o, a, b, start=start, stop=stop, skip_group_check=True)

            def three(o, a_parts, b_parts, start, stop):
                (ah, al), (bh, bl) = a_parts, b_parts
                mm(o, ah, bh, start=start)
                mm(o, ah, bl)
                return mm(o, al, bh, stop=stop)

            pe.wait_ge(w_in, 16 * N_LOADS)
            pe.wait_ge(zeroed, N_ZERO)
            for n in range(2 * G):
                for g in range(G):
                    mm(ps[:, 0, n:n + 1], wqkv[:, g, n * P:(n + 1) * P], n1b[:, g:g + 1],
                       start=(n == 0 and g == 0), stop=(g == 1))
            for e in range(2):
                for p in range(PAIRS):
                    for g in range(G):
                        a = 2 * C + (2 * p + e) * HD
                        mm(ps[HD * p:HD * p + HD, 1 + e, 0:1], wqkv[:, g, a:a + HD], n1b[:, g:g + 1],
                           start=(g == 0), stop=(g == 1))
            for m in range(MT):
                for g in range(G):
                    s = mm(ps[:, 3, m:m + 1], w1[:, g, m * P:(m + 1) * P], n2b[:, g:g + 1],
                           start=(m == 0 and g == 0), stop=(g == 1))
            s.then_inc(setup_pe, 1)
            pe.wait_ge(setup_v, V_BV)
            for e in range(2):
                s = mm(ps[0:1, 4, 0:C], bv[:, e:e + 1], wproj[:, e, :], start=(e == 0), stop=(e == 1))
            s.then_inc(setup_pe, 1)
            pe.wait_ge(setup_v, V_ALL)

            def x_transposes(t, par, post):
                pe.wait_ge(x_in[par], x_count(t, par))
                for n in range(4):
                    bank = X_BANK[n]
                    if n == 0:
                        pe.wait_ge(y_ready, signals(t - 3, 2, 1))
                    elif n == 3:
                        pe.wait_ge(xT_ready, signals(t, 4, 1))
                    elif post:
                        pe.wait_ge(h_ready, signals(t - 2, 2, n))
                    else:
                        pe.wait_ge(k_lo_ready, signals(t - 1, 4, 2 + n))
                    g = n % 2
                    for k in range(4) if n < 2 else [4]:
                        s = pe.transpose(D[bank][:, (k % 4) * P:(k % 4 + 1) * P],
                                         xin[par][:, k, g * P:(g + 1) * P], ident[:])
                    s.then_inc(pe_x, 1)

            def q_product(t, par, g):
                pe.wait_ge(a_hi_ready, signals(t, G, G))
                pe.wait_ge(a_lo_ready, signals(t, G, G))
                pe.wait_ge(gelu_ready, signals(t - 2, MT, 2 + g))
                for kg in range(G):
                    ws = [w[:, kg, g * P:(g + 1) * P] for w in (wqkv_hi, wqkv_lo)]
                    tok = [by_window(a[par], kg)[:, :, 1:1 + TS, 1:1 + TS] for a in (a_hi, a_lo)]
                    s = three(D[Q_BANK[g]], ws, tok, kg == 0, kg == G - 1)
                s.then_inc(pe_q, 1)

            def k_product(t, par, n):
                if n == 0:
                    pe.wait_ge(gelu_ready, signals(t - 2, MT, MT))
                elif n == 3:
                    pe.wait_ge(k_lo_ready, signals(t, 4, 1))
                else:
                    pe.wait_ge(q_lo_ready, signals(t, HEADS, 4 * n))
                g, half = K_PARTS[n]
                o = D[K_BANK[n]][:, 0:HALF]
                for kg in range(G):
                    ws = [w[:, kg, C + g * P:C + (g + 1) * P] for w in (wqkv_hi, wqkv_lo)]
                    s = three(o, ws, [keys(a[par], kg, half) for a in (a_hi, a_lo)], kg == 0, kg == G - 1)
                s.then_inc(pe_k, 1)

            def projection(t, par):
                pe.wait_ge(o_hi_ready, signals(t, TILES, TILES))
                pe.wait_ge(o_lo_ready, signals(t, TILES, TILES))
                for g in range(G):
                    if not isinstance(t, int) or t < BANDS - 1:
                        pe.wait_ge(k_lo_ready, signals(t + 1, 4, 3 + g))
                    o = D[P_BANK[g]]
                    mm(o, bias[:, g * P:(g + 1) * P], ones16[:], start=True)
                    for e in range(2):
                        s = three(o, [w[:, e, g * P:(g + 1) * P] for w in (wproj_hi, wproj_lo)],
                                  [o_[par][:, e, :] for o_ in (o_hi, o_lo)], False, e == 1)
                    s.then_inc(pe_proj, 1)

            def mlp_in(t, m, pre):
                pe.wait_ge(b_hi_ready, signals(t, 1, 1))
                pe.wait_ge(b_lo_ready, signals(t, 1, 1))
                if m == 3:
                    pe.wait_ge(gelu_ready, signals(t, MT, 1))
                elif m == 2:
                    pe.wait_ge(y_ready, signals(t - 1, 2, 2))
                elif pre:
                    pe.wait_ge(xT_ready, signals(t + 2, 4, 3 + m))
                elif m == 1:
                    pe.wait_ge(y_ready, signals(t - 1, 2, 1))
                for g in range(G):
                    s = three(D[IN_BANK[m]], [w[:, g, m * P:(m + 1) * P] for w in (w1_hi, w1_lo)],
                              [b[:, g, :] for b in (b_hi, b_lo)], g == 0, g == G - 1)
                s.then_inc(pe_m1, 1)

            def mlp_out(t, par, n, k, pre, post):
                if n == 1 and k == 0 and pre:
                    pe.wait_ge(xT_ready, signals(t + 3, 4, 2))
                elif n == 1 and k == 0 and post:
                    pe.wait_ge(h_ready, signals(t + 1, 2, 1))
                pe.wait_ge(g_hi_ready, signals(t, MT, MT))
                pe.wait_ge(g_lo_ready, signals(t, MT, MT))
                tok = slice((2 * n + k) * P, (2 * n + k + 1) * P)
                o = D[OUT_BANK[n]][:, k * C:(k + 1) * C]
                mm(o, ones16[:, 0:P], bias[:, C:2 * C], start=(k == 0))
                for m in range(MT):
                    three(o, [g_[:, m, tok] for g_ in (g_hi, g_lo)], [w[:, m, :] for w in (w2_hi, w2_lo)],
                          False, False)
                for g in range(G):
                    s = mm(o[:, g * P:(g + 1) * P], h[par][:, g, tok], ident_ws[:], stop=True)
                s.then_inc(pe_m2, 1)

            def scores(t, par, c):
                pe.wait_ge(maxrow_ready, signals(t, TILES, c))
                if c == 0:
                    pe.wait_ge(mask_in[par], mask_count(t, par))
                    pe.wait_ge(k_lo_ready, signals(t, 4, 2))
                    pe.wait_ge(q_lo_ready, signals(t, HEADS, HEADS))
                if c == 3:
                    pe.wait_ge(k_lo_ready, signals(t, 4, 4))
                mm(ps[:, B_S, 0:PAIRS * NK], qmask[par][:, c, :], key_scores[:].rearrange("p a k -> p (a k)"), start=True)
                for p in range(PAIRS):
                    g = p // 2
                    s = mm(ps[:, B_S, p * NK:(p + 1) * NK],
                           q_hi[par][:, g, c, 2 * (p % 2):2 * (p % 2) + 2, :].rearrange("p h q -> p (h q)"),
                           k_hi[par][:, g, NK * c:NK * (c + 1)], stop=True)
                s.then_inc(pe_s, 1)

            def values(t, par, c):
                pe.wait_ge(v_lo_ready, signals(t, TILES, c))
                for g in range(G):
                    s = three(ps[:, B_V, 0:C], [window(a[par], g, c) for a in (a_hi, a_lo)],
                              [w[:, g, 2 * C:3 * C] for w in (wqkv_hi, wqkv_lo)], g == 0, g == G - 1)
                s.then_inc(pe_v, 1)

            def scores_t(t, par, c):
                if exists(t, c - 2):
                    pe.wait_ge(p_hi_ready, signals(t, TILES, c - 1))
                for g in range(G):
                    o = ps[:, B_ST + c % 2, g * 256:(g + 1) * 256]
                    three(o, [window(k[par], g, c) for k in (k_hi, k_lo)],
                          [q[par][:, g, c].rearrange("p h q -> p (h q)") for q in (q_hi, q_lo)], g == 0, False)

            def max_rows(t, c):
                pe.wait_ge(max_ready, signals(t, TILES, c + 1))
                pe.transpose(ps[:, B_S, PAIRS * NK:PAIRS * NK + P // 2].bitcast(BF16), maxima[c % 2][:], ident16[:]).then_inc(pe_max, 1)

            def mask_t(t, par, c):
                pe.wait_ge(maxrow_ready, signals(t, TILES, c + 1))
                for p in range(PAIRS):
                    s = mm(ps[:, B_ST + c % 2, p * P:(p + 1) * P], key_probs[:, p, :], qmask[par][:, c, :], stop=True)
                s.then_inc(pe_st, 1)

            def weighted(t, c):
                pe.wait_ge(p_lo_ready, signals(t, TILES, c + 1))
                pe.wait_ge(v_lo_ready, signals(t, TILES, c + 1))
                if exists(t, c - 1):
                    pe.wait_ge(o_lo_ready, signals(t, TILES, c))
                b = c % 2
                for p in range(PAIRS):
                    o = ps[:, B_AV, p * VW:(p + 1) * VW]
                    ph, pl = (q[b][0:NK, p * P:(p + 1) * P] for q in (p_hi, p_lo))
                    s = three(o, (ph, pl), (v_hi[b][0:NK, p, :], v_lo[b][0:NK, p, :]), p == 0, True)
                s.then_inc(pe_av, 1)

            def turn(t, c):
                pe.wait_ge(norm_ready, signals(t, TILES, c + 1))
                pe.transpose(ps[:, B_AV, OT_COLS], o_norm[c % 2][:].rearrange("p a d -> p (a d)"), ident[:]
                             ).then_inc(pe_ot, 1)

            def step(t, par, att, pre, post, fin):
                new = old = 1 - par
                for c in range(TILES):
                    ahead = (t, par, c + 1) if c + 1 < TILES else (t + 1, new, 0)
                    more = att if c + 1 < TILES else pre
                    if att:
                        mask_t(t, par, c)
                    if more:
                        scores(*ahead)
                    if exists(t, c - 2):
                        turn(t, c - 2)
                    if att:
                        values(t, par, c)
                    if c in (0, 1) and fin:
                        mlp_out(t - 2, par, 0, c, pre, post)
                    if c == 1 and post:
                        projection(t - 1, old)
                    if c == 1 and pre:
                        x_transposes(t + 1, new, post)
                    if c in (2, 3) and fin:
                        mlp_out(t - 2, par, 1, c - 2, pre, post)
                    if c == 4 and post:
                        for m in range(MT):
                            mlp_in(t - 1, m, pre)
                    if c == 5 and pre:
                        q_product(t + 1, new, 0)
                    if c == 6 and pre:
                        q_product(t + 1, new, 1)
                        k_product(t + 1, new, 0)
                        k_product(t + 1, new, 1)
                    if c == 7 and pre:
                        k_product(t + 1, new, 2)
                        k_product(t + 1, new, 3)
                    if more:
                        max_rows(ahead[0], ahead[2])
                    if exists(t, c - 1):
                        weighted(t, c - 1)
                    if more:
                        scores_t(*ahead)

            run(pe, step)

        @block.vector
        def _(v):
            def zero(ap, value=0.0):
                v.memset(ap, value).then_inc(zeroed, 1)

            for t_ in (*q_hi, *q_lo):
                zero(t_[:].rearrange("p g c h q -> p (g c h q)").bitcast(U32), 0)
            for t_ in qmask:
                zero(t_[:].rearrange("p c q -> p (c q)").bitcast(U32), 0)
            for t_ in xT:
                zero(flat(t_))
            for t_ in maxima:
                zero(t_[:])
            for t_ in v_lo:
                zero(t_[:].rearrange("p a w -> p (a w)"))
            for t_ in v_hi:
                zero(t_[:].rearrange("p a w -> p (a w)"), 1.0)
            for t_ in (*a_hi, *a_lo, *k_hi, *k_lo):
                zero(t_[:, :, TILES * NK:])
            zero(bias[:])
            zero(ones16[:], 1.0)
            v.wait_ge(zeroed, N_ZERO)
            v.wait_ge(w_in, 16 * N_LOADS)

            count = [0]

            def link(ins):
                count[0] += 1
                ins.then_inc(setup_v, 1)
                v.wait_ge(setup_v, count[0])

            v.wait_ge(setup_pe, 1)
            link(v.tensor_tensor(bv[:], bv_in[:], ps[:, 1:3, 0], ALU.add))
            assert count[0] == V_BV
            link(v.tensor_tensor(b1[:], b1_in[:], ps[:, 3, 0:MT], ALU.add))

            def split(hi, lo, src, parts, n):
                for cols, rowf, f in parts:
                    d = wscaled[:, cols]
                    if rowf is None:
                        link(v.tensor_scalar(d, src[:, cols], f, None, ALU.mult))
                    else:
                        link(v.tensor_scalar(d, src[:, cols], rowf, f, ALU.mult, ALU.mult))
                link(v.tensor_copy(hi, wscaled[:, 0:n]))
                link(v.tensor_tensor(lo, wscaled[:, 0:n], hi, ALU.subtract))

            parts = []
            for g in range(G):
                a = g * 3 * C
                parts.append((slice(a, a + C), n1w[:, g:g + 1], WS * HD ** -0.5))
                parts.append((slice(a + C, a + 3 * C), n1w[:, g:g + 1], WS))
            split(flat2(wqkv_hi), flat2(wqkv_lo), flat2(wqkv), parts, G * 3 * C)
            split(flat2(wproj_hi), flat2(wproj_lo), flat2(wproj), [(slice(0, 2 * C), None, WS)], 2 * C)
            split(flat2(w1_hi), flat2(w1_lo), flat2(w1),
                  [(slice(g * HID, (g + 1) * HID), n2w[:, g:g + 1], WS) for g in range(G)], G * HID)
            split(flat2(w2_hi), flat2(w2_lo), flat2(w2), [(slice(0, MT * C), None, WS)], MT * C)
            link(v.tensor_tensor(bqk[:], bqk_in[:], ps[:, 0, 0:2 * G], ALU.add))
            link(v.tensor_scalar(bqk[:, 0:G], bqk[:, 0:G], WS * HD ** -0.5, None, ALU.mult))
            link(v.tensor_scalar(bqk[:, G:2 * G], bqk[:, G:2 * G], WS, None, ALU.mult))
            v.wait_ge(setup_pe, 2)
            link(v.tensor_tensor(brow[:, 0:C], brow_in[:, 0:C], ps[0:1, 4, 0:C], ALU.add))
            link(v.tensor_scalar(brow[:, 0:C], brow[:, 0:C], WS, None, ALU.mult))
            link(v.tensor_scalar(brow[:, C:2 * C], brow_in[:, C:2 * C], WS, None, ALU.mult))
            link(v.tensor_copy(bias[0:1, :], brow[:, :]))
            link(v.tensor_tensor(brow[:, :], brow[:, :], bias[0:1, :], ALU.subtract))
            link(v.tensor_copy(brow16, brow))
            link(v.tensor_copy(bias[32:33, :], brow16))
            link(v.tensor_tensor(brow, brow, brow16, ALU.subtract))
            link(v.tensor_copy(bias[64:65, :], brow[:, :]))
            assert count[0] == V_ALL, count[0]

            def h_from_projection(t, par):
                v.wait_ge(pe_m2, signals(t - 1, 4, 0))
                for g in range(G):
                    v.wait_ge(pe_proj, signals(t, 2, g + 1))
                    v.scalar_tensor_tensor(
                        out=h[par][:, g, :].rearrange("p (i j) -> p i j", j=SIDE),
                        in0=ps[:, P_BANK[g], :].rearrange("p (i j) -> p i j", j=SIDE), scalar=INV,
                        in1=xT[par][:, g, 1:1 + TS, 1:1 + SIDE], op0=ALU.mult, op1=ALU.add).then_inc(h_ready, 1)

            def magnitude(out, of, s):
                v.tensor_single_scalar(out.bitcast(U32), of.bitcast(U32), MAGNITUDE, ALU.bitwise_and).then_inc(s, 1)

            def with_sign(out, sign_of, log, s):
                v.scalar_tensor_tensor(out=out.bitcast(U32), in0=sign_of.bitcast(U32), scalar=SIGN, in1=log.bitcast(U32),
                                       op0=ALU.bitwise_and, op1=ALU.bitwise_or).then_inc(s, 1)

            def x_from_transposes(t, par):
                v.wait_ge(h_ready, signals(t - 2, 2, 2))
                for n in range(4):
                    v.wait_ge(pe_x, signals(t, 4, n + 1))
                    rows = slice(0, TS) if n < 2 else slice(TS, XROWS)
                    size = (rows.stop - rows.start) * SIDE
                    v.tensor_copy(xT[par][:, n % 2, rows, 1:1 + SIDE],
                                  ps[:, X_BANK[n], 0:size].rearrange("p (i j) -> p i j", j=SIDE)).then_inc(xT_ready, 1)

            def q_low(t, par, g):
                for n in range(4):
                    v.wait_ge(q_hi_ready, signals(t, HEADS, 4 * g + n + 1))
                    r = slice(HD * n, HD * n + HD)
                    v.scalar_tensor_tensor(
                        out=q_lo[par][r, g, :, n, :], in0=ps[r, Q_BANK[g], :].rearrange("p (c q) -> p c q", q=NQ),
                        scalar=bqk[r, g:g + 1], in1=q_hi[par][r, g, :, n, :],
                        op0=ALU.add, op1=ALU.subtract).then_inc(q_lo_ready, 1)

            def k_low(t, par, n):
                g, half = K_PARTS[n]
                v.wait_ge(k_hi_ready, signals(t, 4, n + 1))
                v.scalar_tensor_tensor(
                    out=keys(k_lo[par], g, half), in0=ps[:, K_BANK[n], 0:HALF], scalar=bqk[:, G + g:G + g + 1],
                    in1=keys(k_hi[par], g, half), op0=ALU.add, op1=ALU.subtract).then_inc(k_lo_ready, 1)

            def tile_maximum(t, c):
                b = c % 2
                v.wait_ge(pe_s, signals(t, TILES, c + 1))
                v.tensor_reduce(max32[b][:], ps[:, B_S, 0:PAIRS * NK].rearrange("p (a k) -> p a k", k=NK),
                                AX.X, ALU.max).then_inc(max32_ready, 1)
                v.wait_ge(max32_ready, signals(t, TILES, c + 1))
                v.tensor_copy(maxima[b][:, M0:M0 + PAIRS], max32[b][:]).then_inc(max_hi_ready, 1)
                v.wait_ge(max_hi_ready, signals(t, TILES, c + 1))
                v.tensor_tensor(maxima[b][:, M0 + PAIRS:M0 + 2 * PAIRS], max32[b][:], maxima[b][:, M0:M0 + PAIRS],
                                ALU.subtract).then_inc(max_ready, 1)

            def v_low(t, c):
                v.wait_ge(v_hi_ready, signals(t, TILES, c + 1))
                b = c % 2
                v.scalar_tensor_tensor(
                    out=v_lo[b][0:NK, :, 0:2 * HD], in0=ps[0:NK, B_V, 0:C].rearrange("p (a d) -> p a d", d=2 * HD),
                    scalar=INV, in1=v_hi[b][0:NK, :, 0:2 * HD], op0=ALU.mult, op1=ALU.subtract).then_inc(v_lo_ready, 1)

            def maxima_to_mask(t, par, c):
                v.wait_ge(pe_max, signals(t, TILES, c + 1))
                r = slice(M0, M0 + 2 * PAIRS)
                v.tensor_copy(qmask[par][r, c, :],
                              ps[r, B_S, PAIRS * NK:PAIRS * NK + P // 2].bitcast(BF16)).then_inc(maxrow_ready, 1)

            def o_low(t, par, c):
                v.wait_ge(o_hi_ready, signals(t, TILES, c + 1))
                v.tensor_tensor(o_tile(o_lo[par], c), ps_ot(), o_tile(o_hi[par], c), ALU.subtract).then_inc(o_lo_ready, 1)

            def normalise(t, c):
                b = c % 2
                av = ps[:, B_AV, 0:PAIRS * VW].rearrange("p (a w) -> p a w", w=VW)
                v.wait_ge(pe_av, signals(t, TILES, c + 1))
                v.reciprocal(recip[b][:], av[:, :, 2 * HD:VW]).then_inc(recip_ready, 1)
                v.wait_ge(recip_ready, signals(t, TILES, c + 1))
                for e in range(2):
                    r = slice(NQ * e, NQ * e + NQ)
                    s = v.tensor_tensor(o_norm[b][r], av[r, :, HD * e:HD * e + HD],
                                        recip[b][r].to_broadcast([NQ, PAIRS, HD]), ALU.mult)
                s.then_inc(norm_ready, 1)

            def g_high(t, m):
                v.wait_ge(pe_m2, signals(t, 4, 0))
                v.wait_ge(gelu_ready, signals(t, MT, m + 1))
                v.tensor_copy(g_hi[:, m, :], g32[:, m, :]).then_inc(g_hi_ready, 1)

            def step(t, par, att, pre, post, fin):
                new = old = 1 - par
                for c in range(TILES):
                    ahead = (t, par, c + 1) if c + 1 < TILES else (t + 1, new, 0)
                    more = att if c + 1 < TILES else pre
                    if more:
                        tile_maximum(ahead[0], ahead[2])
                    if exists(t, c - 2):
                        o_low(t, par if c >= 2 else old, c - 2)
                    if att:
                        v_low(t, c)
                    if c == 1 and post:
                        h_from_projection(t - 1, old)
                    if c == 1 and pre:
                        x_from_transposes(t + 1, new)
                    if c == 3 and post:
                        v.wait_ge(log2, signals(t - 1, 1, 1))
                        with_sign(ln2_u[:], flat2(h[old]), ln2_s[:], asinh2)
                        v.wait_ge(asinh2, signals(t - 1, 1, 1))
                        v.wait_ge(pe_m1, signals(t - 1, MT, 0))
                        v.tensor_copy(flat2(b_hi), ln2_u[:]).then_inc(b_hi_ready, 1)
                    if c == 4 and pre:
                        v.wait_ge(log1, signals(t + 1, 1, 1))
                        with_sign(ln1_u[:], flat(xT[new]), ln1_s[:], asinh1)
                        v.wait_ge(asinh1, signals(t + 1, 1, 1))
                        for g in range(G):
                            v.tensor_copy(by_window(a_hi[new], g), in_windows(ln1_u, g)).then_inc(a_hi_ready, 1)
                    if c == 5 and pre:
                        q_low(t + 1, new, 0)
                    if c == 6 and pre:
                        q_low(t + 1, new, 1)
                        k_low(t + 1, new, 0)
                        k_low(t + 1, new, 1)
                    if c == 7 and pre:
                        k_low(t + 1, new, 2)
                        k_low(t + 1, new, 3)
                    if more:
                        maxima_to_mask(ahead[0], ahead[1], ahead[2])
                    if c == 1 and post:
                        v.wait_ge(h_ready, signals(t - 1, 2, 2))
                        v.wait_ge(b_lo_ready, signals(t - 1, 1, 0))
                        magnitude(ln2_u[:], flat2(h[old]), abs2)
                    if c == 2 and post:
                        v.wait_ge(abs2, signals(t - 1, 1, 1))
                        v.wait_ge(root2, signals(t - 1, 1, 1))
                        v.tensor_tensor(ln2_u[:], ln2_u[:], ln2_s[:], ALU.add).then_inc(sum2, 1)
                    if exists(t, c - 1):
                        normalise(t, c - 1)
                    if c == 2 and pre:
                        v.wait_ge(xT_ready, signals(t + 1, 4, 4))
                        v.wait_ge(a_lo_ready, signals(t + 1, G, 0))
                        magnitude(ln1_u[:], flat(xT[new]), abs1)
                    if c == 3 and pre:
                        v.wait_ge(abs1, signals(t + 1, 1, 1))
                        v.wait_ge(root1, signals(t + 1, 1, 1))
                        v.tensor_tensor(ln1_u[:], ln1_u[:], ln1_s[:], ALU.add).then_inc(sum1, 1)
                    if c == 5 and post:
                        for m in range(MT):
                            g_high(t - 1, m)

            run(v, step)

        @block.scalar
        def _(act):
            act.wait_ge(zeroed, N_ZERO)
            act.wait_ge(setup_v, V_ALL)

            log_exp_set, gelu_set = "natural_log_exp_and_others", "gelu_and_others"
            act.preload_act_table_set(log_exp_set)

            def square_log(s, of, sq, ln, t):
                act.activation(s, of, ACT.Square).then_inc(sq, 1)
                act.wait_ge(sq, signals(t, 1, 1))
                act.activation(s, s, ACT.Ln, bias=1.0).then_inc(ln, 1)

            def root(s, ln, rt, t):
                act.wait_ge(ln, signals(t, 1, 1))
                act.activation(s, s, ACT.Exp, scale=0.5).then_inc(rt, 1)

            def q_high(t, par, g):
                act.wait_ge(pe_q, signals(t, 2, g + 1))
                for n in range(4):
                    r = slice(HD * n, HD * n + HD)
                    act.activation(q_hi[par][r, g, :, n, :], ps[r, Q_BANK[g], :].rearrange("p (c q) -> p c q", q=NQ),
                                   ACT.Identity, bias=bqk[r, g:g + 1]).then_inc(q_hi_ready, 1)

            def k_high(t, par, n):
                g, half = K_PARTS[n]
                act.wait_ge(pe_k, signals(t, 4, n + 1))
                act.activation(keys(k_hi[par], g, half), ps[:, K_BANK[n], 0:HALF],
                               ACT.Identity, bias=bqk[:, G + g:G + g + 1]).then_inc(k_hi_ready, 1)

            def result(t, n):
                act.wait_ge(pe_m2, signals(t, 4, 2 * n + 2))
                act.wait_ge(y_out[n], signals(t, 16, 0))
                act.activation(flat2(y[n]), ps[:, OUT_BANK[n], :], ACT.Copy, scale=INV).then_inc(y_ready, 1)

            def v_high(t, c):
                act.wait_ge(pe_v, signals(t, TILES, c + 1))
                if exists(t, c - 2):
                    act.wait_ge(pe_av, signals(t, TILES, c - 1))
                act.activation(v_hi[c % 2][0:NK, :, 0:2 * HD], ps[0:NK, B_V, 0:C].rearrange("p (a d) -> p a d", d=2 * HD),
                               ACT.Copy, scale=INV).then_inc(v_hi_ready, 1)

            def o_high(t, par, c):
                act.wait_ge(pe_ot, signals(t, TILES, c + 1))
                if c == 0:
                    act.wait_ge(pe_proj, signals(t - 1, 2, 0))
                act.activation(o_tile(o_hi[par], c), ps_ot(), ACT.Copy).then_inc(o_hi_ready, 1)

            def probabilities(t, c):
                b = c % 2
                act.wait_ge(pe_st, signals(t, TILES, c + 1))
                if exists(t, c - 2):
                    act.wait_ge(p_lo_ready, signals(t, TILES, c - 1))
                act.activation(prob[b][0:NK], ps[0:NK, B_ST + b, :], ACT.Exp, scale=INV * INV).then_inc(prob_ready, 1)
                act.activation(p_hi[b][0:NK], ps[0:NK, B_ST + b, :], ACT.Exp, scale=INV * INV).then_inc(p_hi_ready, 1)

            def gelus(t):
                act.preload_act_table_set(gelu_set)
                act.wait_ge(g_lo_ready, signals(t, MT, 0))
                for m in range(MT):
                    act.wait_ge(pe_m1, signals(t, MT, m + 1))
                    act.activation(g32[:, m, :], ps[:, IN_BANK[m], :], ACT.Gelu, bias=b1[:, m:m + 1],
                                   scale=INV).then_inc(gelu_ready, 1)
                act.preload_act_table_set(log_exp_set)

            def step(t, par, att, pre, post, fin):
                new = old = 1 - par
                for c in range(TILES):
                    if att:
                        probabilities(t, c)
                    if exists(t, c - 2):
                        o_high(t, par if c >= 2 else old, c - 2)
                    if att:
                        v_high(t, c)
                    if c == 1 and fin:
                        result(t - 2, 0)
                    if c == 4 and fin:
                        result(t - 2, 1)
                    if c == 1 and post:
                        act.wait_ge(h_ready, signals(t - 1, 2, 2))
                        act.wait_ge(asinh2, signals(t - 1, 1, 0))
                        square_log(ln2_s[:], flat2(h[old]), sq2, ln2a, t - 1)
                    if c == 2 and post:
                        root(ln2_s[:], ln2a, root2, t - 1)
                    if c == 2 and pre:
                        act.wait_ge(xT_ready, signals(t + 1, 4, 4))
                        act.wait_ge(asinh1, signals(t + 1, 1, 0))
                        square_log(ln1_s[:], flat(xT[new]), sq1, ln1a, t + 1)
                    if c == 3 and post:
                        act.wait_ge(sum2, signals(t - 1, 1, 1))
                        act.activation(ln2_s[:], ln2_u[:], ACT.Ln).then_inc(log2, 1)
                    if c == 3 and pre:
                        root(ln1_s[:], ln1a, root1, t + 1)
                    if c == 4 and pre:
                        act.wait_ge(sum1, signals(t + 1, 1, 1))
                        act.activation(ln1_s[:], ln1_u[:], ACT.Ln).then_inc(log1, 1)
                    if c == 4 and post:
                        gelus(t - 1)
                    if c == 5 and pre:
                        q_high(t + 1, new, 0)
                    if c == 6 and pre:
                        q_high(t + 1, new, 1)
                        k_high(t + 1, new, 0)
                        k_high(t + 1, new, 1)
                    if c == 7 and pre:
                        k_high(t + 1, new, 2)
                        k_high(t + 1, new, 3)

            run(act, step)

        @block.gpsimd
        def _(pool):
            def p_low(t, c):
                pool.wait_ge(p_hi_ready, signals(t, TILES, c + 1))
                if exists(t, c - 2):
                    pool.wait_ge(pe_av, signals(t, TILES, c - 1))
                b = c % 2
                pool.tensor_tensor(p_lo[b][0:NK], prob[b][0:NK], p_hi[b][0:NK], ALU.subtract).then_inc(p_lo_ready, 1)

            def g_low(t, m):
                pool.wait_ge(g_hi_ready, signals(t, MT, m + 1))
                pool.tensor_tensor(g_lo[:, m, :], g32[:, m, :], g_hi[:, m, :], ALU.subtract).then_inc(g_lo_ready, 1)

            def step(t, par, att, pre, post, fin):
                new = 1 - par
                for c in range(TILES):
                    if att:
                        p_low(t, c)
                    if c == 3 and post:
                        pool.wait_ge(b_hi_ready, signals(t - 1, 1, 1))
                        pool.tensor_tensor(flat2(b_lo), ln2_u[:], flat2(b_hi), ALU.subtract).then_inc(b_lo_ready, 1)
                    if c == 4 and pre:
                        for g in range(G):
                            pool.wait_ge(a_hi_ready, signals(t + 1, G, g + 1))
                            pool.tensor_tensor(by_window(a_lo[new], g), in_windows(ln1_u, g), by_window(a_hi[new], g),
                                               ALU.subtract).then_inc(a_lo_ready, 1)
                    if c == 5 and post:
                        g_low(t - 1, 0)
                    if c == 6 and post:
                        g_low(t - 1, 1)
                        g_low(t - 1, 2)
                    if c == 7 and post:
                        g_low(t - 1, 3)

            run(pool, step)


_INS = ["x", "qkv_w", "qkv_b", "proj_w", "proj_b", "n1_w", "n1_b", "n2_w", "n2_b", "mlp_w1", "mlp_b1", "mlp_w2", "mlp_b2"]


def kernel(**inputs):
    import concourse.bacc as _bacc
    from concourse.bass_utils import run_bass_kernel_spmd as _run

    nc = _bacc.Bacc("TRN2", target_bir_lowering=False, num_devices=1)
    arrays, args = {}, []
    given = [(n, np.ascontiguousarray(inputs[n if n == "x" else "L0_conv_" + n])) for n in _INS]
    for name, a in given + list(constants().items()):
        arrays[f"in_{name}_dram"] = a
        args.append(nc.dram_tensor(f"in_{name}_dram", a.shape, mybir.dt.from_np(a.dtype), kind="ExternalInput").ap())
    args.append(nc.dram_tensor("out_dram", (IMAGES, SIDE, SIDE, C), F32, kind="ExternalOutput").ap())
    build(nc, *args)
    r = _run(nc, [arrays], core_ids=[0])
    return r.results[0]["out_dram"]
```

```python
from contextlib import ExitStack

import numpy as np

import concourse.bass as bass
from concourse import mybir

ALU = mybir.AluOpType
ACT = mybir.ActivationFunctionType
F32 = mybir.dt.float32
F16 = mybir.dt.float16
BF16 = mybir.dt.bfloat16
U32 = mybir.dt.uint32
AX = mybir.AxisListType

P = 128
IMAGES, SIDE, C = 16, 64, 256
HEADS = 8
HD = C // HEADS
HID = 2 * C
G = C // P
PAIRS = HEADS // 2
TS = 8
WIN = TS + 2
NK = WIN * WIN
NQ = TS * TS
TILES = SIDE // TS
BPI = SIDE // TS
BANDS = IMAGES * BPI
TOK = TS * SIDE
XROWS = WIN
XTOK = XROWS * SIDE
PITCH = SIDE + 2
PADTOK = XROWS * PITCH
HALF = TILES // 2 * NK
VW = 2 * HD + 1
MT = HID // P
WS = 16.0
INV = 1.0 / WS
M0 = 32
MASKED_Q, MASKED_K = -32768.0, 32768.0
KPAD = P - NK
SIGN, MAGNITUDE = 0x80000000, 0x7FFFFFFF

N_LOADS = 15 + 2 * PAIRS
N_ZERO = 22
V_BV, V_ALL = 1, 23

B_S, B_ST, B_V, B_AV = 3, 4, 6, 7
OT_COLS = slice(3 * P, 4 * P)
P_BANK = [1, 2]
X_BANK = [0, 1, 2]
OUT_BANK = [0, 1]
IN_BANK = [2, 0, 1, 2]
Q_BANK = [0, 2]
K_PARTS = [(0, 0), (1, 0), (0, 1), (1, 1)]
K_BANK = [1, 0, 1, 2]


def bfloat16_bits(a):
    return (np.ascontiguousarray(a, np.float32).view(np.uint32) >> 16).astype(np.uint16)


def constants():
    ident = np.eye(P, dtype=np.float32)
    marks = np.zeros((P, WIN, WIN), np.float32)
    for r in range(WIN):
        marks[r, r, :] = MASKED_K
        marks[WIN + r, :, r] = MASKED_K
    marks = marks.reshape(P, 1, NK)
    key_scores = np.repeat(marks, PAIRS, axis=1)
    key_probs = np.concatenate([key_scores, np.zeros((P, PAIRS, KPAD), np.float32)], axis=2)
    for p in range(PAIRS):
        key_probs[[M0 + p, M0 + PAIRS + p], p, :NK] = -1.0
    query = np.zeros((BPI, 2 * WIN, TILES, 2, TS, TS), np.float32)
    for b in range(BPI):
        for q in range(TS):
            first = min(max(TS * b + q - 1, 0), SIDE - 3)
            for r in range(WIN):
                if not first <= TS * b - 1 + r < first + 3:
                    query[b, r, :, :, q, :] = MASKED_Q
    for c in range(TILES):
        for q in range(TS):
            first = min(max(TS * c + q - 1, 0), SIDE - 3)
            for r in range(WIN):
                if not first <= TS * c - 1 + r < first + 3:
                    query[:, WIN + r, c, :, :, q] = MASKED_Q
    return {
        "ident": ident,
        "ident16": bfloat16_bits(np.eye(P)),
        "key_scores": bfloat16_bits(key_scores.reshape(P, PAIRS * NK)),
        "key_probs": bfloat16_bits(key_probs.reshape(P, PAIRS * P)),
        "query_mask": bfloat16_bits(query.reshape(BPI, 2 * WIN, TILES * P)),
    }


def build(nc, x, qkv_w, qkv_b, proj_w, proj_b, n1_w, n1_b, n2_w, n2_b, mlp_w1, mlp_b1, mlp_w2, mlp_b2,
          ident_c, ident16_c, key_scores_c, key_probs_c, query_mask_c, out):
    x_rows = x.rearrange("i r j c -> (i r j) c")
    out_rows = out.rearrange("i r j c -> (i r j) c")

    with ExitStack() as ctx:
        def sb(name, shape, dt):
            return ctx.enter_context(nc.sbuf_tensor(name, shape, dt))

        def sem(name):
            return ctx.enter_context(nc.semaphore(name))

        ps = ctx.enter_context(nc.psum_tensor("ps", [P, 8, 512], F32))

        ident = sb("ident", [P, P], F32)
        ident16 = sb("ident16", [P, P], BF16)
        key_scores = sb("key_scores", [P, PAIRS, NK], BF16)
        key_probs = sb("key_probs", [P, PAIRS, P], BF16)
        wqkv = sb("wqkv", [P, G, 3 * C], F32)
        wproj = sb("wproj", [P, 2, C], F32)
        w1 = sb("w1", [P, G, HID], F32)
        w2 = sb("w2", [P, MT, C], F32)
        wqkv_hi, wqkv_lo = sb("wqkv_hi", [P, G, 3 * C], F16), sb("wqkv_lo", [P, G, 3 * C], F16)
        wproj_hi, wproj_lo = sb("wproj_hi", [P, 2, C], F16), sb("wproj_lo", [P, 2, C], F16)
        w1_hi, w1_lo = sb("w1_hi", [P, G, HID], F16), sb("w1_lo", [P, G, HID], F16)
        w2_hi, w2_lo = sb("w2_hi", [P, MT, C], F16), sb("w2_lo", [P, MT, C], F16)
        n1w, n1b = sb("n1w", [P, G], F32), sb("n1b", [P, G], F32)
        n2w, n2b = sb("n2w", [P, G], F32), sb("n2b", [P, G], F32)
        bv_in, bv = sb("bv_in", [P, 2], F32), sb("bv", [P, 2], F32)
        b1_in, b1 = sb("b1_in", [P, MT], F32), sb("b1", [P, MT], F32)
        bqk_in, bqk = sb("bqk_in", [P, 2 * G], F32), sb("bqk", [P, 2 * G], F32)
        bp_in, bp = sb("bp_in", [P, G], F32), sb("bp", [P, G], F32)
        b2 = sb("b2", [P, C], F32)

        xin = [sb(f"xin{i}", [P, XTOK // P, C], F32) for i in range(2)]
        xT = [sb(f"xT{i}", [P, G, XROWS, PITCH], F32) for i in range(2)]
        x_kept = sb("x_kept", [P, G, TOK], F32)
        a_hi = [sb(f"a_hi{i}", [P, G, TILES * NK + KPAD], F16) for i in range(2)]
        a_lo = [sb(f"a_lo{i}", [P, G, TILES * NK + KPAD], F16) for i in range(2)]
        k_hi = [sb(f"k_hi{i}", [P, G, TILES * NK + KPAD], F16) for i in range(2)]
        k_lo = [sb(f"k_lo{i}", [P, G, TILES * NK + KPAD], F16) for i in range(2)]
        q_hi = [sb(f"q_hi{i}", [P, G, TILES, 4, NQ], F16) for i in range(2)]
        q_lo = [sb(f"q_lo{i}", [P, G, TILES, 4, NQ], F16) for i in range(2)]
        qmask = [sb(f"qmask{i}", [P, TILES, P], BF16) for i in range(2)]
        o_hi = [sb(f"o_hi{i}", [P, 2, TOK], F16) for i in range(2)]
        o_lo = [sb(f"o_lo{i}", [P, 2, TOK], F16) for i in range(2)]
        v_hi = [sb(f"v_hi{i}", [P, PAIRS, VW], F16) for i in range(2)]
        v_lo = [sb(f"v_lo{i}", [P, PAIRS, VW], F16) for i in range(2)]
        prob = [sb(f"prob{i}", [P, 512], F32) for i in range(2)]
        p_hi = [sb(f"p_hi{i}", [P, 512], F16) for i in range(2)]
        p_lo = [sb(f"p_lo{i}", [P, 512], F16) for i in range(2)]
        max32 = [sb(f"max32{i}", [P, PAIRS], F32) for i in range(2)]
        maxima = [sb(f"maxima{i}", [P, P], BF16) for i in range(2)]
        recip = [sb(f"recip{i}", [P, PAIRS, 1], F32) for i in range(2)]
        o_norm = [sb(f"o_norm{i}", [P, PAIRS, HD], F32) for i in range(2)]
        ln1_s, ln1_u = sb("ln1_s", [P, G * PADTOK], F32), sb("ln1_u", [P, G * PADTOK], F32)
        ln2_s, ln2_u = sb("ln2_s", [P, G * TOK], F32), sb("ln2_u", [P, G * TOK], F32)
        h = [sb(f"h{i}", [P, G, TOK], F32) for i in range(2)]
        b_hi, b_lo = sb("b_hi", [P, G, TOK], F16), sb("b_lo", [P, G, TOK], F16)
        g32 = sb("g32", [P, MT, TOK], F32)
        g_hi, g_lo = sb("g_hi", [P, MT, TOK], F16), sb("g_lo", [P, MT, TOK], F16)
        y = [sb(f"y{i}", [P, 2, C], F32) for i in range(2)]
        wscaled = sb("wscaled", [P, G * 3 * C], F32)

        w_in = sem("w_in")
        x_in = [sem("x_in0"), sem("x_in1")]
        edge_in = sem("edge_in")
        mask_in = [sem("mask_in0"), sem("mask_in1")]
        y_out = [sem("y_out0"), sem("y_out1")]
        zeroed, setup_v, setup_pe = sem("zeroed"), sem("setup_v"), sem("setup_pe")
        pe_x, pe_q, pe_k, pe_proj, pe_m1, pe_m2 = (sem("pe_" + s) for s in ("x", "q", "k", "proj", "m1", "m2"))
        pe_s, pe_v, pe_max, pe_st, pe_av, pe_ot = (sem("pe_" + s) for s in ("s", "v", "max", "st", "av", "ot"))
        xT_ready, h_ready, abs1, abs2, sum1, sum2 = (sem("dve_" + s) for s in ("xT", "h", "abs1", "abs2", "sum1", "sum2"))
        asinh1, asinh2, a_hi_ready, b_hi_ready = (sem("dve_" + s) for s in ("asinh1", "asinh2", "a_hi", "b_hi"))
        q_lo_ready, k_lo_ready, g_hi_ready = (sem("dve_" + s) for s in ("q_lo", "k_lo", "g_hi"))
        max32_ready, max_hi_ready, max_ready = (sem("dve_" + s) for s in ("max32", "max_hi", "max"))
        v_lo_ready, maxrow_ready = sem("dve_v_lo"), sem("dve_maxrow")
        recip_ready, norm_ready, o_lo_ready = (sem("dve_" + s) for s in ("recip", "norm", "o_lo"))
        sq1, ln1a, root1, log1, sq2, ln2a, root2, log2 = (
            sem("act_" + s) for s in ("sq1", "ln1a", "root1", "log1", "sq2", "ln2a", "root2", "log2"))
        q_hi_ready, k_hi_ready, gelu_ready, y_ready = (sem("act_" + s) for s in ("q_hi", "k_hi", "gelu", "y"))
        v_hi_ready, prob_ready, p_hi_ready, o_hi_ready = (sem("act_" + s) for s in ("v_hi", "prob", "p_hi", "o_hi"))
        a_lo_ready, b_lo_ready, g_lo_ready, p_lo_ready = (sem("pool_" + s) for s in ("a_lo", "b_lo", "g_lo", "p_lo"))
        y_biased, x_kept_ready = sem("pool_y"), sem("act_x_kept")

        block = ctx.enter_context(nc.Block())

        def flat(t):
            return t[:].rearrange("p g r c -> p (g r c)")

        def flat2(t):
            return t[:].rearrange("p g n -> p (g n)")

        def o_tile(o, c):
            return o[:].rearrange("p e (i c j) -> p e c i j", c=TILES, j=TS)[:, :, c % TILES]

        def ps_ot():
            return ps[:, B_AV, OT_COLS].rearrange("p (e i j) -> p e i j", e=2, j=TS)

        def exists(t, c):
            return not isinstance(t, int) or 0 <= TILES * t + c < TILES * BANDS

        def signals(t, per, n):
            return max(t * per + n, 0) if isinstance(t, int) else t * per + n

        def run(eng, step):
            step(-1, 1, False, True, False, False)
            step(0, 0, True, True, False, False)
            step(1, 1, True, True, True, False)
            with eng.Fori(0, (BANDS - 4) // 2) as i:
                step(i * 2 + 2, 0, True, True, True, True)
                step(i * 2 + 3, 1, True, True, True, True)
            step(BANDS - 2, 0, True, True, True, True)
            step(BANDS - 1, 1, True, False, True, True)
            step(BANDS, 0, False, False, True, True)
            step(BANDS + 1, 1, False, False, False, True)

        def window(t, g, c):
            return t[:, g, NK * c:NK * c + P]

        def keys(t, g, half):
            return t[:, g, half * HALF:(half + 1) * HALF]

        def by_window(t, g):
            return t[:, g, 0:TILES * NK].rearrange("p (c r j) -> p c r j", r=WIN, j=WIN)

        def in_windows(u, g):
            a = u[:, g * PADTOK:(g + 1) * PADTOK]
            return bass.AP(a.tensor, a.offset, [list(a.ap[0]), [TS, TILES], [PITCH, WIN], [1, WIN]])

        @block.sync
        def _(sp):
            loads = [
                (ident[:], ident_c), (ident16[:], ident16_c.bitcast(BF16)),
                (key_scores[:].rearrange("p a k -> p (a k)"), key_scores_c.bitcast(BF16)),
                (key_probs[:].rearrange("p a k -> p (a k)"), key_probs_c.bitcast(BF16)),
                (wqkv[:], qkv_w.rearrange("(g p) n -> p g n", p=P)),
                (w1[:], mlp_w1.rearrange("(g p) n -> p g n", p=P)),
                (w2[:], mlp_w2.rearrange("(m p) n -> p m n", p=P)),
                (n1w[:], n1_w.rearrange("(g p) -> p g", p=P)), (n1b[:], n1_b.rearrange("(g p) -> p g", p=P)),
                (n2w[:], n2_w.rearrange("(g p) -> p g", p=P)), (n2b[:], n2_b.rearrange("(g p) -> p g", p=P)),
                (b1_in[:], mlp_b1.rearrange("(m p) -> p m", p=P)),
                (bqk_in[:], qkv_b[0:2 * C].rearrange("(n p) -> p n", p=P)),
                (bp_in[:], proj_b.rearrange("(g p) -> p g", p=P)),
                (b2[:], bass.AP(mlp_b2.tensor, mlp_b2.offset, [[0, P], [1, C]])),
            ]
            wp = proj_w.rearrange("(p e d) n -> p d e n", p=PAIRS, e=2)
            bvp = qkv_b[2 * C:3 * C].rearrange("(p e d) -> p d e", p=PAIRS, e=2)
            for p in range(PAIRS):
                loads.append((wproj[HD * p:HD * p + HD], wp[p]))
                loads.append((bv_in[HD * p:HD * p + HD], bvp[p]))
            assert len(loads) == N_LOADS
            for to, of in loads:
                sp.dma_start(to, of, allow_slow_non_contiguous=True).then_inc(w_in, 16)

            def load_x(t, par):
                sp.dma_start(xin[par][:], x_rows[bass.ds(t * TOK - SIDE, XTOK)].rearrange("(k p) c -> p k c", p=P)
                             ).then_inc(x_in[par], 16)

            def load_edge_x(t, par):
                above = t == 0
                beyond = 0 if above else XROWS - 1
                tiles = slice(1, XTOK // P) if above else slice(0, XTOK // P - 1)
                beside = 1 if above else XROWS - 2
                edge = t * TOK if above else (t + 1) * TOK - SIDE
                for slot in (beyond, beside):
                    at = slot * SIDE
                    sp.dma_start(xin[par][at % P:at % P + SIDE, at // P, :], x_rows[edge:edge + SIDE]).then_inc(edge_in, 16)
                sp.wait_ge(edge_in, 32 if above else 64)
                first = t * TOK - SIDE + tiles.start * P
                sp.dma_start(xin[par][:, tiles, :], x_rows[first:first + 4 * P].rearrange("(k p) c -> p k c", p=P)
                             ).then_inc(x_in[par], 16)

            def load_mask(t, par, b):
                sp.dma_start(qmask[par][0:2 * WIN].rearrange("k c q -> k (c q)"), query_mask_c[b].bitcast(BF16)).then_inc(mask_in[par], 16)

            def store_y(t, par):
                for n in range(2):
                    sp.wait_ge(y_biased, signals(t, 2, n + 1))
                    dst = out_rows[bass.ds(t * TOK + n * 2 * P, 2 * P)]
                    sp.dma_start(dst.rearrange("(k p) c -> p k c", p=P), y[n][:]).then_inc(y_out[n], 16)

            sp.wait_ge(zeroed, N_ZERO)
            load_edge_x(0, 0)
            load_mask(0, 0, 0)
            load_x(1, 1)
            load_mask(1, 1, 1)

            def step(t, par, stores=True):
                sp.wait_ge(pe_x, signals(t, 3, 0))
                load_x(t + 1, 1 - par)
                sp.wait_ge(pe_st, signals(t, TILES, 0))
                load_mask(t + 1, 1 - par, (t + 1) % BPI)
                if stores:
                    store_y(t - 2, par)

            step(1, 1, False)
            with sp.Fori(0, (BANDS - 4) // 2) as i:
                step(i * 2 + 2, 0)
                step(i * 2 + 3, 1)
            sp.wait_ge(pe_x, signals(BANDS - 2, 3, 0))
            load_edge_x(BANDS - 1, 1)
            sp.wait_ge(pe_st, signals(BANDS - 2, TILES, 0))
            load_mask(BANDS - 1, 1, BPI - 1)
            for t in range(BANDS - 4, BANDS):
                store_y(t, t % 2)
            for n in range(2):
                sp.wait_ge(y_out[n], 16 * BANDS)

        def x_count(t, par):
            return (t // 2) * 16 + 16

        def mask_count(t, par):
            return (t // 2) * 16 + 16

        @block.tensor
        def _(pe):
            D = [ps[:, n, :] for n in range(3)]

            def mm(o, a, b, start=False, stop=False):
                return pe.matmul(o, a, b, start=start, stop=stop, skip_group_check=True)

            def three(o, a_parts, b_parts, start, stop):
                (ah, al), (bh, bl) = a_parts, b_parts
                mm(o, ah, bh, start=start)
                mm(o, ah, bl)
                return mm(o, al, bh, stop=stop)

            pe.wait_ge(w_in, 16 * N_LOADS)
            pe.wait_ge(zeroed, N_ZERO)
            for n in range(2 * G):
                for g in range(G):
                    mm(ps[:, 0, n:n + 1], wqkv[:, g, n * P:(n + 1) * P], n1b[:, g:g + 1],
                       start=(n == 0 and g == 0), stop=(g == 1))
            for e in range(2):
                for p in range(PAIRS):
                    for g in range(G):
                        a = 2 * C + (2 * p + e) * HD
                        mm(ps[HD * p:HD * p + HD, 1 + e, 0:1], wqkv[:, g, a:a + HD], n1b[:, g:g + 1],
                           start=(g == 0), stop=(g == 1))
            for m in range(MT):
                for g in range(G):
                    s = mm(ps[:, 3, m:m + 1], w1[:, g, m * P:(m + 1) * P], n2b[:, g:g + 1],
                           start=(m == 0 and g == 0), stop=(g == 1))
            s.then_inc(setup_pe, 1)
            pe.wait_ge(setup_v, V_BV)
            for g in range(G):
                for e in range(2):
                    s = mm(ps[:, 4, g:g + 1], wproj[:, e, g * P:(g + 1) * P], bv[:, e:e + 1],
                           start=(g == 0 and e == 0), stop=(e == 1))
            s.then_inc(setup_pe, 1)
            pe.wait_ge(setup_v, V_ALL)

            def x_transposes(t, par):
                pe.wait_ge(x_in[par], x_count(t, par))
                for n in range(3):
                    pe.wait_ge(k_lo_ready, signals(t - 1, 4, 2 + n))
                    for k, g in [(k, n) for k in range(4)] if n < 2 else [(4, g) for g in range(G)]:
                        at = (k if n < 2 else g) * P
                        s = pe.transpose(D[X_BANK[n]][:, at:at + P], xin[par][:, k, g * P:(g + 1) * P], ident[:])
                    s.then_inc(pe_x, 1)

            def q_product(t, par, g):
                pe.wait_ge(a_hi_ready, signals(t, G, G))
                pe.wait_ge(a_lo_ready, signals(t, G, G))
                pe.wait_ge(gelu_ready, signals(t - 2, MT, 2 + 2 * g))
                for kg in range(G):
                    ws = [w[:, kg, g * P:(g + 1) * P] for w in (wqkv_hi, wqkv_lo)]
                    tok = [by_window(a[par], kg)[:, :, 1:1 + TS, 1:1 + TS] for a in (a_hi, a_lo)]
                    s = three(D[Q_BANK[g]], ws, tok, kg == 0, kg == G - 1)
                s.then_inc(pe_q, 1)

            def k_product(t, par, n):
                pe.wait_ge(a_hi_ready, signals(t, G, G))
                pe.wait_ge(a_lo_ready, signals(t, G, G))
                if n == 0:
                    pe.wait_ge(gelu_ready, signals(t - 2, MT, 3))
                elif n == 2:
                    pe.wait_ge(k_lo_ready, signals(t, 4, 1))
                else:
                    pe.wait_ge(q_lo_ready, signals(t, HEADS, 4 if n == 1 else 8))
                g, half = K_PARTS[n]
                o = D[K_BANK[n]][:, 0:HALF]
                for kg in range(G):
                    ws = [w[:, kg, C + g * P:C + (g + 1) * P] for w in (wqkv_hi, wqkv_lo)]
                    s = three(o, ws, [keys(a[par], kg, half) for a in (a_hi, a_lo)], kg == 0, kg == G - 1)
                s.then_inc(pe_k, 1)

            def projection(t, par, pre):
                pe.wait_ge(o_hi_ready, signals(t, TILES, TILES))
                pe.wait_ge(o_lo_ready, signals(t, TILES, TILES))
                for g in range(G):
                    if pre:
                        pe.wait_ge(xT_ready, signals(t + 2, 3, 2 + g))
                    else:
                        pe.wait_ge(k_lo_ready, signals(BANDS - 1, 4, 3 + g))
                    o = D[P_BANK[g]]
                    for e in range(2):
                        s = three(o, [w[:, e, g * P:(g + 1) * P] for w in (wproj_hi, wproj_lo)],
                                  [o_[par][:, e, :] for o_ in (o_hi, o_lo)], e == 0, e == 1)
                    s.then_inc(pe_proj, 1)

            def mlp_in(t, m):
                if m == 3:
                    pe.wait_ge(gelu_ready, signals(t, MT, 1))
                elif m in (1, 2):
                    pe.wait_ge(y_ready, signals(t - 1, 2, m))
                for g in range(G):
                    pe.wait_ge(b_hi_ready, signals(t, G, g + 1))
                    pe.wait_ge(b_lo_ready, signals(t, G, g + 1))
                    s = three(D[IN_BANK[m]], [w[:, g, m * P:(m + 1) * P] for w in (w1_hi, w1_lo)],
                              [b[:, g, :] for b in (b_hi, b_lo)], g == 0, g == G - 1)
                s.then_inc(pe_m1, 1)

            def mlp_out(t, par, n, k, pre, post):
                if k == 0 and n == 1:
                    if post:
                        pe.wait_ge(h_ready, signals(t + 1, 2, 1))
                elif k == 0 and pre:
                    pe.wait_ge(xT_ready, signals(t + 3, 3, 1))
                elif k == 0:
                    pe.wait_ge(k_lo_ready, signals(BANDS - 1, 4, 2))
                pe.wait_ge(g_hi_ready, signals(t, MT, MT))
                pe.wait_ge(g_lo_ready, signals(t, MT, MT))
                tok = slice((2 * n + k) * P, (2 * n + k + 1) * P)
                o = D[OUT_BANK[n]][:, k * C:(k + 1) * C]
                for g in range(G):
                    pe.matmul(o[:, g * P:(g + 1) * P], h[par][:, g, tok], ident[:], start=(k == 0 and g == 0),
                              stop=False, is_transpose=True, skip_group_check=True)
                for m in range(MT):
                    s = three(o, [g_[:, m, tok] for g_ in (g_hi, g_lo)], [w[:, m, :] for w in (w2_hi, w2_lo)],
                              False, m == MT - 1)
                s.then_inc(pe_m2, 1)

            def scores(t, par, c):
                pe.wait_ge(maxrow_ready, signals(t, TILES, c))
                if c == 0:
                    pe.wait_ge(mask_in[par], mask_count(t, par))
                    pe.wait_ge(k_lo_ready, signals(t, 4, 2))
                    pe.wait_ge(q_lo_ready, signals(t, HEADS, HEADS))
                if c == 3:
                    pe.wait_ge(k_lo_ready, signals(t, 4, 4))
                mm(ps[:, B_S, 0:PAIRS * NK], qmask[par][:, c, :], key_scores[:].rearrange("p a k -> p (a k)"), start=True)
                for p in range(PAIRS):
                    g = p // 2
                    s = mm(ps[:, B_S, p * NK:(p + 1) * NK],
                           q_hi[par][:, g, c, 2 * (p % 2):2 * (p % 2) + 2, :].rearrange("p h q -> p (h q)"),
                           k_hi[par][:, g, NK * c:NK * (c + 1)], stop=True)
                s.then_inc(pe_s, 1)

            def values(t, par, c):
                pe.wait_ge(v_lo_ready, signals(t, TILES, c))
                for g in range(G):
                    s = three(ps[:, B_V, 0:C], [window(a[par], g, c) for a in (a_hi, a_lo)],
                              [w[:, g, 2 * C:3 * C] for w in (wqkv_hi, wqkv_lo)], g == 0, g == G - 1)
                s.then_inc(pe_v, 1)

            def scores_t(t, par, c):
                if exists(t, c - 2):
                    pe.wait_ge(p_hi_ready, signals(t, TILES, c - 1))
                for g in range(G):
                    o = ps[:, B_ST + c % 2, g * 256:(g + 1) * 256]
                    three(o, [window(k[par], g, c) for k in (k_hi, k_lo)],
                          [q[par][:, g, c].rearrange("p h q -> p (h q)") for q in (q_hi, q_lo)], g == 0, False)

            def max_rows(t, c):
                pe.wait_ge(max_ready, signals(t, TILES, c + 1))
                pe.transpose(ps[:, B_S, PAIRS * NK:PAIRS * NK + P // 2].bitcast(BF16), maxima[c % 2][:], ident16[:]).then_inc(pe_max, 1)

            def mask_t(t, par, c):
                pe.wait_ge(maxrow_ready, signals(t, TILES, c + 1))
                for p in range(PAIRS):
                    s = mm(ps[:, B_ST + c % 2, p * P:(p + 1) * P], key_probs[:, p, :], qmask[par][:, c, :], stop=True)
                s.then_inc(pe_st, 1)

            def weighted(t, c):
                pe.wait_ge(p_lo_ready, signals(t, TILES, c + 1))
                pe.wait_ge(v_lo_ready, signals(t, TILES, c + 1))
                if exists(t, c - 1):
                    pe.wait_ge(o_lo_ready, signals(t, TILES, c))
                b = c % 2
                for p in range(PAIRS):
                    o = ps[:, B_AV, p * VW:(p + 1) * VW]
                    ph, pl = (q[b][0:NK, p * P:(p + 1) * P] for q in (p_hi, p_lo))
                    s = three(o, (ph, pl), (v_hi[b][0:NK, p, :], v_lo[b][0:NK, p, :]), p == 0, True)
                s.then_inc(pe_av, 1)

            def turn(t, c):
                pe.wait_ge(norm_ready, signals(t, TILES, c + 1))
                pe.transpose(ps[:, B_AV, OT_COLS], o_norm[c % 2][:].rearrange("p a d -> p (a d)"), ident[:]
                             ).then_inc(pe_ot, 1)

            def step(t, par, att, pre, post, fin):
                new = old = 1 - par
                for c in range(TILES):
                    ahead = (t, par, c + 1) if c + 1 < TILES else (t + 1, new, 0)
                    more = att if c + 1 < TILES else pre
                    if att:
                        mask_t(t, par, c)
                    if c + 1 < TILES and more:
                        scores(*ahead)
                    if exists(t, c - 2):
                        turn(t, c - 2)
                    if att:
                        values(t, par, c)
                    if c == 0 and pre:
                        x_transposes(t + 1, new)
                    if c == 1 and post:
                        projection(t - 1, old, pre)
                    if c in (2, 3) and fin:
                        mlp_out(t - 2, par, c - 2, 0, pre, post)
                        mlp_out(t - 2, par, c - 2, 1, pre, post)
                    if c == 4 and post:
                        for m in range(MT):
                            mlp_in(t - 1, m)
                    if c == 4 and pre:
                        q_product(t + 1, new, 0)
                    if c == 5 and pre:
                        k_product(t + 1, new, 0)
                        q_product(t + 1, new, 1)
                    if c == 6 and pre:
                        k_product(t + 1, new, 1)
                    if c == 7 and pre:
                        k_product(t + 1, new, 2)
                        scores(*ahead)
                        k_product(t + 1, new, 3)
                    if c + 1 < TILES and more:
                        max_rows(ahead[0], ahead[2])
                    if exists(t, c - 1):
                        weighted(t, c - 1)
                    if c + 1 == TILES and more:
                        max_rows(ahead[0], ahead[2])
                    if more:
                        scores_t(*ahead)

            run(pe, step)

        @block.vector
        def _(v):
            def zero(ap, value=0.0):
                v.memset(ap, value).then_inc(zeroed, 1)

            for t_ in (*q_hi, *q_lo):
                zero(t_[:].rearrange("p g c h q -> p (g c h q)").bitcast(U32), 0)
            for t_ in qmask:
                zero(t_[:].rearrange("p c q -> p (c q)").bitcast(U32), 0)
            for t_ in xT:
                zero(flat(t_))
            for t_ in maxima:
                zero(t_[:])
            for t_ in v_lo:
                zero(t_[:].rearrange("p a w -> p (a w)"))
            for t_ in v_hi:
                zero(t_[:].rearrange("p a w -> p (a w)"), 1.0)
            for t_ in (*a_hi, *a_lo, *k_hi, *k_lo):
                zero(t_[:, :, TILES * NK:])
            v.wait_ge(zeroed, N_ZERO)
            v.wait_ge(w_in, 16 * N_LOADS)

            count = [0]

            def link(ins):
                count[0] += 1
                ins.then_inc(setup_v, 1)
                v.wait_ge(setup_v, count[0])

            v.wait_ge(setup_pe, 1)
            link(v.tensor_tensor(bv[:], bv_in[:], ps[:, 1:3, 0], ALU.add))
            assert count[0] == V_BV
            link(v.tensor_tensor(b1[:], b1_in[:], ps[:, 3, 0:MT], ALU.add))

            def split(hi, lo, src, parts, n):
                for cols, rowf, f in parts:
                    d = wscaled[:, cols]
                    if rowf is None:
                        link(v.tensor_scalar(d, src[:, cols], f, None, ALU.mult))
                    else:
                        link(v.tensor_scalar(d, src[:, cols], rowf, f, ALU.mult, ALU.mult))
                link(v.tensor_copy(hi, wscaled[:, 0:n]))
                link(v.tensor_tensor(lo, wscaled[:, 0:n], hi, ALU.subtract))

            parts = []
            for g in range(G):
                a = g * 3 * C
                parts.append((slice(a, a + C), n1w[:, g:g + 1], WS * HD ** -0.5))
                parts.append((slice(a + C, a + 3 * C), n1w[:, g:g + 1], WS))
            split(flat2(wqkv_hi), flat2(wqkv_lo), flat2(wqkv), parts, G * 3 * C)
            split(flat2(wproj_hi), flat2(wproj_lo), flat2(wproj), [(slice(0, 2 * C), None, WS)], 2 * C)
            split(flat2(w1_hi), flat2(w1_lo), flat2(w1),
                  [(slice(g * HID, (g + 1) * HID), n2w[:, g:g + 1], WS) for g in range(G)], G * HID)
            split(flat2(w2_hi), flat2(w2_lo), flat2(w2), [(slice(0, MT * C), None, WS)], MT * C)
            link(v.tensor_tensor(bqk[:], bqk_in[:], ps[:, 0, 0:2 * G], ALU.add))
            link(v.tensor_scalar(bqk[:, 0:G], bqk[:, 0:G], WS * HD ** -0.5, None, ALU.mult))
            link(v.tensor_scalar(bqk[:, G:2 * G], bqk[:, G:2 * G], WS, None, ALU.mult))
            v.wait_ge(setup_pe, 2)
            link(v.tensor_tensor(bp[:], bp_in[:], ps[:, 4, 0:G], ALU.add))
            link(v.tensor_scalar(bp[:], bp[:], WS, None, ALU.mult))
            assert count[0] == V_ALL, count[0]

            def h_from_projection(t, par):
                v.wait_ge(pe_m2, signals(t - 1, 4, 0))
                v.wait_ge(x_kept_ready, signals(t, 1, 1))
                for g in range(G):
                    v.wait_ge(pe_proj, signals(t, 2, g + 1))
                    v.scalar_tensor_tensor(
                        out=h[par][:, g, :].rearrange("p (i j) -> p i j", j=SIDE),
                        in0=ps[:, P_BANK[g], :].rearrange("p (i j) -> p i j", j=SIDE), scalar=bp[:, g:g + 1],
                        in1=x_kept[:, g, :].rearrange("p (i j) -> p i j", j=SIDE), op0=ALU.add, op1=ALU.add).then_inc(h_ready, 1)

            def magnitude(out, of, s):
                v.tensor_single_scalar(out.bitcast(U32), of.bitcast(U32), MAGNITUDE, ALU.bitwise_and).then_inc(s, 1)

            def with_sign(out, sign_of, log, s):
                v.scalar_tensor_tensor(out=out.bitcast(U32), in0=sign_of.bitcast(U32), scalar=SIGN, in1=log.bitcast(U32),
                                       op0=ALU.bitwise_and, op1=ALU.bitwise_or).then_inc(s, 1)

            def x_from_transposes(t, par, part):
                v.wait_ge(x_kept_ready, signals(t - 2, 1, 1))
                v.wait_ge(pe_x, signals(t, 3, part + 1))
                if part < 2:
                    v.tensor_scalar(xT[par][:, part, 0:TS, 1:1 + SIDE],
                                    ps[:, X_BANK[part], :].rearrange("p (i j) -> p i j", j=SIDE), WS, None, ALU.mult).then_inc(xT_ready, 1)
                else:
                    v.tensor_scalar(xT[par][:, :, TS:XROWS, 1:1 + SIDE],
                                    ps[:, X_BANK[2], 0:G * P].rearrange("p (g i j) -> p g i j", g=G, j=SIDE),
                                    WS, None, ALU.mult).then_inc(xT_ready, 1)

            def q_low(t, par, g, heads=range(4)):
                for n in heads:
                    v.wait_ge(q_hi_ready, signals(t, HEADS, 4 * g + n + 1))
                    r = slice(HD * n, HD * n + HD)
                    v.scalar_tensor_tensor(
                        out=q_lo[par][r, g, :, n, :], in0=ps[r, Q_BANK[g], :].rearrange("p (c q) -> p c q", q=NQ),
                        scalar=bqk[r, g:g + 1], in1=q_hi[par][r, g, :, n, :],
                        op0=ALU.add, op1=ALU.subtract).then_inc(q_lo_ready, 1)

            def k_low(t, par, n):
                g, half = K_PARTS[n]
                v.wait_ge(k_hi_ready, signals(t, 4, n + 1))
                v.scalar_tensor_tensor(
                    out=keys(k_lo[par], g, half), in0=ps[:, K_BANK[n], 0:HALF], scalar=bqk[:, G + g:G + g + 1],
                    in1=keys(k_hi[par], g, half), op0=ALU.add, op1=ALU.subtract).then_inc(k_lo_ready, 1)

            def maximum(t, c):
                v.wait_ge(pe_s, signals(t, TILES, c + 1))
                v.tensor_reduce(max32[c % 2][:], ps[:, B_S, 0:PAIRS * NK].rearrange("p (a k) -> p a k", k=NK),
                                AX.X, ALU.max).then_inc(max32_ready, 1)

            def maximum_high(t, c):
                v.wait_ge(max32_ready, signals(t, TILES, c + 1))
                v.tensor_copy(maxima[c % 2][:, M0:M0 + PAIRS], max32[c % 2][:]).then_inc(max_hi_ready, 1)

            def maximum_low(t, c):
                b = c % 2
                v.wait_ge(max_hi_ready, signals(t, TILES, c + 1))
                v.tensor_tensor(maxima[b][:, M0 + PAIRS:M0 + 2 * PAIRS], max32[b][:], maxima[b][:, M0:M0 + PAIRS],
                                ALU.subtract).then_inc(max_ready, 1)

            def v_low(t, c):
                v.wait_ge(v_hi_ready, signals(t, TILES, c + 1))
                b = c % 2
                v.scalar_tensor_tensor(
                    out=v_lo[b][0:NK, :, 0:2 * HD], in0=ps[0:NK, B_V, 0:C].rearrange("p (a d) -> p a d", d=2 * HD),
                    scalar=INV, in1=v_hi[b][0:NK, :, 0:2 * HD], op0=ALU.mult, op1=ALU.subtract).then_inc(v_lo_ready, 1)

            def maxima_to_mask(t, par, c):
                v.wait_ge(pe_max, signals(t, TILES, c + 1))
                r = slice(M0, M0 + 2 * PAIRS)
                v.tensor_copy(qmask[par][r, c, :],
                              ps[r, B_S, PAIRS * NK:PAIRS * NK + P // 2].bitcast(BF16)).then_inc(maxrow_ready, 1)

            def o_low(t, par, c):
                v.wait_ge(o_hi_ready, signals(t, TILES, c + 1))
                v.tensor_tensor(o_tile(o_lo[par], c), ps_ot(), o_tile(o_hi[par], c), ALU.subtract).then_inc(o_lo_ready, 1)

            def sum_reciprocal(t, c):
                v.wait_ge(pe_av, signals(t, TILES, c + 1))
                av = ps[:, B_AV, 0:PAIRS * VW].rearrange("p (a w) -> p a w", w=VW)
                v.reciprocal(recip[c % 2][:], av[:, :, 2 * HD:VW]).then_inc(recip_ready, 1)

            def normalise(t, c):
                b = c % 2
                av = ps[:, B_AV, 0:PAIRS * VW].rearrange("p (a w) -> p a w", w=VW)
                v.wait_ge(recip_ready, signals(t, TILES, c + 1))
                for e in range(2):
                    r = slice(NQ * e, NQ * e + NQ)
                    s = v.tensor_tensor(o_norm[b][r], av[r, :, HD * e:HD * e + HD],
                                        recip[b][r].to_broadcast([NQ, PAIRS, HD]), ALU.mult)
                s.then_inc(norm_ready, 1)

            def b_high(t, g):
                v.wait_ge(asinh2, signals(t, 1, 1))
                v.wait_ge(pe_m1, signals(t, MT, 0))
                v.tensor_copy(b_hi[:, g, :], ln2_u[:, g * TOK:(g + 1) * TOK]).then_inc(b_hi_ready, 1)

            def g_high(t, m):
                v.wait_ge(pe_m2, signals(t, 4, 0))
                v.wait_ge(gelu_ready, signals(t, MT, m + 1))
                v.tensor_copy(g_hi[:, m, :], g32[:, m, :]).then_inc(g_hi_ready, 1)

            def step(t, par, att, pre, post, fin):
                new = old = 1 - par
                for c in range(TILES):
                    last = c + 1 == TILES
                    t_ahead, par_ahead, c_ahead = (t + 1, new, 0) if last else (t, par, c + 1)
                    more = pre if last else att
                    turned = exists(t, c - 2)
                    par_turned = par if c >= 2 else old
                    if c == 1 and turned:
                        o_low(t, par_turned, c - 2)
                    if last:
                        if turned:
                            o_low(t, par_turned, c - 2)
                        if att:
                            v_low(t, c)
                    if more:
                        maximum(t_ahead, c_ahead)
                    if c in (3, 4) and turned:
                        o_low(t, par_turned, c - 2)
                    if c == 5 and pre:
                        q_low(t + 1, new, 0, (0,))
                    if c == 6 and pre:
                        k_low(t + 1, new, 0)
                    if more:
                        maximum_high(t_ahead, c_ahead)
                    if c == 2 and turned:
                        o_low(t, par_turned, c - 2)
                    if c in (3, 4) and att:
                        v_low(t, c)
                    if c == 5 and pre:
                        q_low(t + 1, new, 0, (1,))
                    if c == 6 and pre:
                        q_low(t + 1, new, 1, (0,))
                    if more:
                        maximum_low(t_ahead, c_ahead)
                    if c in (0, 5, 6) and turned:
                        o_low(t, par_turned, c - 2)
                    if c == 0 and pre:
                        x_from_transposes(t + 1, new, 0)
                        x_from_transposes(t + 1, new, 1)
                    if c in (1, 5) and att:
                        v_low(t, c)
                    if c == 1 and pre:
                        v.wait_ge(xT_ready, signals(t + 1, 3, 3))
                        v.wait_ge(a_lo_ready, signals(t + 1, G, 0))
                        magnitude(ln1_u[:], flat(xT[new]), abs1)
                    if c == 1 and post:
                        h_from_projection(t - 1, old)
                    if c == 2 and post:
                        v.wait_ge(abs2, signals(t - 1, 1, 1))
                        v.wait_ge(root2, signals(t - 1, 1, 1))
                        v.scalar_tensor_tensor(out=ln2_u[:], in0=ln2_u[:], scalar=INV, in1=ln2_s[:],
                                               op0=ALU.mult, op1=ALU.add).then_inc(sum2, 1)
                    if c == 3 and post:
                        v.wait_ge(log2, signals(t - 1, 1, 1))
                        with_sign(ln2_u[:], flat2(h[old]), ln2_s[:], asinh2)
                    if c == 4 and post:
                        for m in range(MT):
                            g_high(t - 1, m)
                    if c == 5 and pre:
                        q_low(t + 1, new, 0, (2,))
                    if c == 6 and pre:
                        q_low(t + 1, new, 1, (1,))
                    if c == 7 and pre:
                        k_low(t + 1, new, 2)
                    if more:
                        maxima_to_mask(t_ahead, par_ahead, c_ahead)
                    if c == 3 and post:
                        b_high(t - 1, 0)
                    if exists(t, c - 1):
                        sum_reciprocal(t, c - 1)
                    if c == 0 and pre:
                        x_from_transposes(t + 1, new, 2)
                    if c == 3 and post:
                        b_high(t - 1, 1)
                    if att and c in (6,):
                        v_low(t, c)
                    if exists(t, c - 1):
                        normalise(t, c - 1)
                    if c == 0 and att:
                        v_low(t, c)
                    if att and c == 2:
                        v_low(t, c)
                    if c == 1 and pre:
                        v.wait_ge(abs1, signals(t + 1, 1, 1))
                        v.wait_ge(root1, signals(t + 1, 1, 1))
                        v.scalar_tensor_tensor(out=ln1_u[:], in0=ln1_u[:], scalar=INV, in1=ln1_s[:],
                                               op0=ALU.mult, op1=ALU.add).then_inc(sum1, 1)
                    if c == 1 and post:
                        v.wait_ge(h_ready, signals(t - 1, 2, 2))
                        v.wait_ge(b_lo_ready, signals(t - 1, G, 0))
                        magnitude(ln2_u[:], flat2(h[old]), abs2)
                    if c == 2 and pre:
                        v.wait_ge(log1, signals(t + 1, 1, 1))
                        with_sign(ln1_u[:], flat(xT[new]), ln1_s[:], asinh1)
                    if c == 3 and pre:
                        v.wait_ge(asinh1, signals(t + 1, 1, 1))
                        for g in range(G):
                            v.tensor_copy(by_window(a_hi[new], g), in_windows(ln1_u, g)).then_inc(a_hi_ready, 1)
                    if c == 5 and pre:
                        q_low(t + 1, new, 0, (3,))
                    if c == 6 and pre:
                        q_low(t + 1, new, 1, (2, 3))
                        k_low(t + 1, new, 1)
                    if c == 7 and pre:
                        k_low(t + 1, new, 3)

            run(v, step)

        @block.scalar
        def _(act):
            act.wait_ge(zeroed, N_ZERO)
            act.wait_ge(setup_v, V_ALL)

            log_exp_set, gelu_set = "natural_log_exp_and_others", "gelu_and_others"
            act.preload_act_table_set(log_exp_set)

            def root(s, ln, rt, t):
                act.wait_ge(ln, signals(t, 1, 1))
                act.activation(s, s, ACT.Exp, scale=0.5).then_inc(rt, 1)

            def q_high(t, par, g, heads=range(4)):
                act.wait_ge(pe_q, signals(t, 2, g + 1))
                for n in heads:
                    r = slice(HD * n, HD * n + HD)
                    act.activation(q_hi[par][r, g, :, n, :], ps[r, Q_BANK[g], :].rearrange("p (c q) -> p c q", q=NQ),
                                   ACT.Identity, bias=bqk[r, g:g + 1]).then_inc(q_hi_ready, 1)

            def k_high(t, par, n):
                g, half = K_PARTS[n]
                act.wait_ge(pe_k, signals(t, 4, n + 1))
                act.activation(keys(k_hi[par], g, half), ps[:, K_BANK[n], 0:HALF],
                               ACT.Identity, bias=bqk[:, G + g:G + g + 1]).then_inc(k_hi_ready, 1)

            def result(t, n):
                act.wait_ge(pe_m2, signals(t, 4, 2 * n + 2))
                act.wait_ge(y_out[n], signals(t, 16, 0))
                act.activation(flat2(y[n]), ps[:, OUT_BANK[n], :], ACT.Copy, scale=INV).then_inc(y_ready, 1)

            def v_high(t, c):
                act.wait_ge(pe_v, signals(t, TILES, c + 1))
                if exists(t, c - 2):
                    act.wait_ge(pe_av, signals(t, TILES, c - 1))
                act.activation(v_hi[c % 2][0:NK, :, 0:2 * HD], ps[0:NK, B_V, 0:C].rearrange("p (a d) -> p a d", d=2 * HD),
                               ACT.Copy, scale=INV).then_inc(v_hi_ready, 1)

            def o_high(t, par, c):
                act.wait_ge(pe_ot, signals(t, TILES, c + 1))
                if c == 0:
                    act.wait_ge(pe_proj, signals(t - 1, 2, 0))
                act.activation(o_tile(o_hi[par], c), ps_ot(), ACT.Copy).then_inc(o_hi_ready, 1)

            def probabilities(t, c):
                b = c % 2
                act.wait_ge(pe_st, signals(t, TILES, c + 1))
                if exists(t, c - 2):
                    act.wait_ge(p_lo_ready, signals(t, TILES, c - 1))
                act.activation(prob[b][0:NK], ps[0:NK, B_ST + b, :], ACT.Exp, scale=INV * INV).then_inc(prob_ready, 1)
                act.activation(p_hi[b][0:NK], ps[0:NK, B_ST + b, :], ACT.Exp, scale=INV * INV).then_inc(p_hi_ready, 1)

            def gelus(t):
                act.preload_act_table_set(gelu_set)
                act.wait_ge(g_lo_ready, signals(t, MT, 0))
                for m in range(MT):
                    act.wait_ge(pe_m1, signals(t, MT, m + 1))
                    act.activation(g32[:, m, :], ps[:, IN_BANK[m], :], ACT.Gelu, bias=b1[:, m:m + 1],
                                   scale=INV).then_inc(gelu_ready, 1)
                act.preload_act_table_set(log_exp_set)

            def step(t, par, att, pre, post, fin):
                new = old = 1 - par
                for c in range(TILES):
                    if att and c != 1:
                        probabilities(t, c)
                    if exists(t, c - 2):
                        o_high(t, par if c >= 2 else old, c - 2)
                    if att and c == 1:
                        probabilities(t, c)
                    if c == 2 and post:
                        root(ln2_s[:], ln2a, root2, t - 1)
                    if att:
                        v_high(t, c)
                    if c == 0 and pre:
                        act.wait_ge(xT_ready, signals(t + 1, 3, 3))
                        act.wait_ge(asinh1, signals(t + 1, 1, 0))
                        act.activation(ln1_s[:], flat(xT[new]), ACT.Square, scale=INV).then_inc(sq1, 1)
                    if c == 1 and pre:
                        act.wait_ge(sq1, signals(t + 1, 1, 1))
                        act.activation(ln1_s[:], ln1_s[:], ACT.Ln, bias=1.0).then_inc(ln1a, 1)
                        root(ln1_s[:], ln1a, root1, t + 1)
                    if c == 1 and post:
                        act.wait_ge(h_ready, signals(t - 1, 2, 2))
                        act.wait_ge(asinh2, signals(t - 1, 1, 0))
                        act.activation(ln2_s[:], flat2(h[old]), ACT.Square, scale=INV).then_inc(sq2, 1)
                        act.wait_ge(sq2, signals(t - 1, 1, 1))
                        act.activation(ln2_s[:], ln2_s[:], ACT.Ln, bias=1.0).then_inc(ln2a, 1)
                    if c == 2 and pre:
                        act.wait_ge(sum1, signals(t + 1, 1, 1))
                        act.activation(ln1_s[:], ln1_u[:], ACT.Ln).then_inc(log1, 1)
                    if c == 2 and post:
                        act.wait_ge(sum2, signals(t - 1, 1, 1))
                        act.activation(ln2_s[:], ln2_u[:], ACT.Ln).then_inc(log2, 1)
                    if c in (3, 4) and fin:
                        result(t - 2, c - 3)
                    if c == 4 and post:
                        gelus(t - 1)
                    if c == 4 and pre:
                        q_high(t + 1, new, 0, (0, 1))
                    if c == 5 and pre:
                        q_high(t + 1, new, 0, (2, 3))
                        k_high(t + 1, new, 0)
                        q_high(t + 1, new, 1)
                    if c == 6 and pre:
                        k_high(t + 1, new, 1)
                    if c == 7 and pre:
                        k_high(t + 1, new, 2)
                        k_high(t + 1, new, 3)
                    if c == 6 and att:
                        act.wait_ge(h_ready, signals(t - 1, 2, 2))
                        act.wait_ge(xT_ready, signals(t, 3, 3))
                        act.activation(x_kept[:].rearrange("p g (i j) -> p g i j", j=SIDE),
                                       xT[par][:, :, 1:1 + TS, 1:1 + SIDE], ACT.Copy).then_inc(x_kept_ready, 1)

            run(act, step)

        @block.gpsimd
        def _(pool):
            def p_low(t, c):
                pool.wait_ge(p_hi_ready, signals(t, TILES, c + 1))
                if exists(t, c - 2):
                    pool.wait_ge(pe_av, signals(t, TILES, c - 1))
                b = c % 2
                pool.tensor_tensor(p_lo[b][0:NK], prob[b][0:NK], p_hi[b][0:NK], ALU.subtract).then_inc(p_lo_ready, 1)

            def g_low(t, m):
                pool.wait_ge(g_hi_ready, signals(t, MT, m + 1))
                pool.tensor_tensor(g_lo[:, m, :], g32[:, m, :], g_hi[:, m, :], ALU.subtract).then_inc(g_lo_ready, 1)

            def bias_y(t, n):
                pool.wait_ge(y_ready, signals(t, 2, n + 1))
                pool.tensor_tensor(y[n][:], y[n][:], b2[:].rearrange("p (a c) -> p a c", a=1).to_broadcast([P, 2, C]),
                                   ALU.add).then_inc(y_biased, 1)

            def step(t, par, att, pre, post, fin):
                new = 1 - par
                for c in range(TILES):
                    if att:
                        p_low(t, c)
                    if c == 3 and post:
                        for g in range(G):
                            pool.wait_ge(b_hi_ready, signals(t - 1, G, g + 1))
                            pool.tensor_tensor(b_lo[:, g, :], ln2_u[:, g * TOK:(g + 1) * TOK], b_hi[:, g, :],
                                               ALU.subtract).then_inc(b_lo_ready, 1)
                    if c == 4 and pre:
                        for g in range(G):
                            pool.wait_ge(a_hi_ready, signals(t + 1, G, g + 1))
                            pool.tensor_tensor(by_window(a_lo[new], g), in_windows(ln1_u, g), by_window(a_hi[new], g),
                                               ALU.subtract).then_inc(a_lo_ready, 1)
                    if c in (4, 5) and fin:
                        bias_y(t - 2, c - 4)
                    if c >= 4 and post:
                        g_low(t - 1, c - 4)

            run(pool, step)


_INS = ["x", "qkv_w", "qkv_b", "proj_w", "proj_b", "n1_w", "n1_b", "n2_w", "n2_b", "mlp_w1", "mlp_b1", "mlp_w2", "mlp_b2"]


def kernel(**inputs):
    import concourse.bacc as _bacc
    from concourse.bass_utils import run_bass_kernel_spmd as _run

    nc = _bacc.Bacc("TRN2", target_bir_lowering=False, num_devices=1)
    arrays, args = {}, []
    given = [(n, np.ascontiguousarray(inputs[n if n == "x" else "L0_conv_" + n])) for n in _INS]
    for name, a in given + list(constants().items()):
        arrays[f"in_{name}_dram"] = a
        args.append(nc.dram_tensor(f"in_{name}_dram", a.shape, mybir.dt.from_np(a.dtype), kind="ExternalInput").ap())
    args.append(nc.dram_tensor("out_dram", (IMAGES, SIDE, SIDE, C), F32, kind="ExternalOutput").ap())
    build(nc, *args)
    r = _run(nc, [arrays], core_ids=[0])
    return r.results[0]["out_dram"]
```
